# Optimizing a Trainium2 kernel written in Bass

```python
import numpy as np
import jax
import jax.numpy as jnp

def _softmax(x, axis=-1):
    return jax.nn.softmax(x, axis=axis)

def _gelu(x):
    return jax.nn.gelu(x, approximate=True)

def _silu(x):
    return jax.nn.silu(x)

def _sigmoid(x):
    return jax.nn.sigmoid(x)

def _layernorm(x, axis=-1, eps=1e-05):
    m = jnp.mean(x, axis=axis, keepdims=True)
    v = jnp.var(x, axis=axis, keepdims=True)
    return (x - m) / jnp.sqrt(v + eps)

def _scatter_add(tgt, idx, src, axis=0):
    return tgt.at[idx].add(src)

def _segment_sum(src, seg, n):
    return jax.ops.segment_sum(src, seg, n)
kernel_name = 'mk_xattn_ffn_d1_seqx_r4_1de65c'

def setup_inputs(seed: int=0):
    np.random.seed(seed)
    _w = jnp.asarray

    def _rec_inputs():
        import jax
        import jax.numpy as jnp
        _rk = jax.random.key(seed)
        x = -0.0003929 + 0.9999 * jax.random.normal(jax.random.fold_in(_rk, 1), (32, 128, 1024), jnp.float32)
        _lenS = 128 - jax.random.randint(jax.random.fold_in(_rk, 7), (32,), 0, max(1, 128 // 4) + 1, jnp.int32)
        _lenS2 = 128 - jax.random.randint(jax.random.fold_in(_rk, 8), (32,), 0, max(1, 128 // 4) + 1, jnp.int32)
        _ctx_4096P = jax.random.normal(jax.random.fold_in(_rk, 11), (32, 16, 1024), jnp.float32)
        _ctx_4096c = jax.random.dirichlet(jax.random.fold_in(_rk, 511), 0.3 * jnp.ones((16,), jnp.float32), (32, 128))
        _ctx_4096t = jnp.einsum('bsk,bkd->bsd', _ctx_4096c, _ctx_4096P)
        _ctx_4096t = _ctx_4096t * jax.lax.rsqrt(jnp.mean(jnp.square(_ctx_4096t)) + 1e-12) * 0.953939
        ctx_4096 = 2.81802e-05 + 1.00001 * (_ctx_4096t + 0.3 * jax.random.normal(jax.random.fold_in(_rk, 611), (32, 128, 1024), jnp.float32))
        return (x, ctx_4096)
    x, ctx_4096 = _rec_inputs()

    def _L0_xattn_setup():
        import jax, jax.numpy as jnp
        import numpy as np
        DIM = 128
        HEADS = 8
        DIM_HEAD = 64
        HIDDEN = HEADS * DIM_HEAD
        SCALE = DIM_HEAD ** (-0.5)
        key = jax.random.key(seed)
        ks = jax.random.split(key, 9)
        b, n = (8, 1024)
        std = 1.0 / np.sqrt(DIM)
        return {'q': jax.random.normal(ks[0], (b, DIM, n), jnp.float32), 'k': jax.random.normal(ks[1], (b, DIM, n), jnp.float32), 'v': jax.random.normal(ks[2], (b, DIM, n), jnp.float32), 'Wq': jax.random.normal(ks[3], (HIDDEN, DIM), jnp.float32) * std, 'Wk': jax.random.normal(ks[4], (HIDDEN, DIM), jnp.float32) * std, 'Wv': jax.random.normal(ks[5], (HIDDEN, DIM), jnp.float32) * std, 'Wo': jax.random.normal(ks[6], (DIM, HIDDEN), jnp.float32) * (1.0 / np.sqrt(HIDDEN)), 'bo': jax.random.normal(ks[7], (DIM,), jnp.float32) * 0.01, 'g': jnp.ones((1, DIM, 1), jnp.float32)}
    _L0_xattn_all = _L0_xattn_setup()
    _L0_xattn_in = {k: v for k, v in _L0_xattn_all.items() if k in ('Wq', 'Wk', 'Wv', 'Wo', 'bo', 'g')}
    del _L0_xattn_all

    def _L0_ffn_setup():
        import jax, jax.numpy as jnp
        import numpy as np
        OUT, IN = (1024, 1024)
        GROUP = 64
        NUM_GROUPS = OUT * IN // GROUP

        def _dequantize_4bit(weight_q4, weight_scale):
            low = weight_q4 & 15
            high = weight_q4 >> 4 & 15
            q8 = jnp.stack([low, high], axis=-1).reshape(weight_q4.shape[0], -1)
            x_norm = q8.astype(jnp.float32) / 15.0
            return x_norm * (2.0 * weight_scale) - weight_scale
        key = jax.random.key(seed)
        k1, k2, k3, k4 = jax.random.split(key, 4)
        x = jax.random.normal(k1, (4, 512, IN), dtype=jnp.float32)
        weight_q4 = jax.random.randint(k2, (NUM_GROUPS, GROUP // 2), 0, 64, dtype=jnp.int32)
        weight_scale = jax.random.uniform(k3, (NUM_GROUPS, 1), dtype=jnp.float32)
        bias = jax.random.normal(k4, (OUT,), dtype=jnp.float32)
        return {'x': x, 'weight_q4': weight_q4, 'weight_scale': weight_scale, 'bias': bias}
    _L0_ffn_all = _L0_ffn_setup()
    _L0_ffn_in = {k: v for k, v in _L0_ffn_all.items() if k in ('weight_q4', 'weight_scale', 'bias')}
    del _L0_ffn_all
    return {'x': x, 'ctx_4096': ctx_4096, 'L0_xattn_Wq': _L0_xattn_in['Wq'], 'L0_xattn_Wk': _L0_xattn_in['Wk'], 'L0_xattn_Wv': _L0_xattn_in['Wv'], 'L0_xattn_Wo': _L0_xattn_in['Wo'], 'L0_xattn_bo': _L0_xattn_in['bo'], 'L0_xattn_g': _L0_xattn_in['g'], 'L0_ffn_weight_q4': _L0_ffn_in['weight_q4'], 'L0_ffn_weight_scale': _L0_ffn_in['weight_scale'], 'L0_ffn_bias': _L0_ffn_in['bias']}

def reference(x, ctx_4096, L0_xattn_Wq, L0_xattn_Wk, L0_xattn_Wv, L0_xattn_Wo, L0_xattn_bo, L0_xattn_g, L0_ffn_weight_q4, L0_ffn_weight_scale, L0_ffn_bias):
    import jax
    import jax.numpy as jnp

    def _L0_xattn_ref(q, k, v, Wq, Wk, Wv, Wo, bo, g):
        import jax, jax.numpy as jnp
        import numpy as np
        DIM = 128
        HEADS = 8
        DIM_HEAD = 64
        HIDDEN = HEADS * DIM_HEAD
        SCALE = DIM_HEAD ** (-0.5)
        b = q.shape[0]
        qh = jnp.einsum('bcn,oc->bon', q, Wq).reshape(b, HEADS, DIM_HEAD, -1)
        kh = jnp.einsum('bcn,oc->bon', k, Wk).reshape(b, HEADS, DIM_HEAD, -1)
        vh = jnp.einsum('bcn,oc->bon', v, Wv).reshape(b, HEADS, DIM_HEAD, -1)
        qh = jax.nn.softmax(qh, axis=-2) * SCALE
        kh = jax.nn.softmax(kh, axis=-1)
        context = jnp.einsum('bhdn,bhen->bhde', kh, vh)
        out = jnp.einsum('bhde,bhdn->bhen', context, qh)
        out = out.reshape(b, HIDDEN, -1)
        out = jnp.einsum('bcn,oc->bon', out, Wo) + bo[None, :, None]
        norm = jnp.maximum(jnp.sqrt(jnp.sum(out * out, axis=1, keepdims=True)), 1e-12)
        return out / norm * g * np.sqrt(DIM)

    def _L0_ffn_ref(x, weight_q4, weight_scale, bias):
        import jax, jax.numpy as jnp
        import numpy as np
        OUT, IN = (1024, 1024)
        GROUP = 64
        NUM_GROUPS = OUT * IN // GROUP

        def _dequantize_4bit(weight_q4, weight_scale):
            low = weight_q4 & 15
            high = weight_q4 >> 4 & 15
            q8 = jnp.stack([low, high], axis=-1).reshape(weight_q4.shape[0], -1)
            x_norm = q8.astype(jnp.float32) / 15.0
            return x_norm * (2.0 * weight_scale) - weight_scale
        w = _dequantize_4bit(weight_q4, weight_scale).reshape(OUT, IN)
        return jnp.einsum('bsi,oi->bso', x, w) + bias
    x = x + _L0_xattn_ref(_layernorm(x, axis=-1), ctx_4096, ctx_4096, L0_xattn_Wq, L0_xattn_Wk, L0_xattn_Wv, L0_xattn_Wo, L0_xattn_bo, L0_xattn_g)
    x = x + _L0_ffn_ref(_layernorm(x, axis=-1), L0_ffn_weight_q4, L0_ffn_weight_scale, L0_ffn_bias)
    return x

_drawn_inputs = setup_inputs


def setup_inputs(seed=0):
    import zlib

    import numpy as np

    out = dict(_drawn_inputs(seed))
    spreads = {'L0_xattn_g': (1.0, 0.2)}
    factors = {}
    for name, (base, spread) in spreads.items():
        noise = np.random.default_rng([zlib.crc32(name.encode()), seed]).standard_normal(out[name].shape)
        drawn = base * np.exp(spread * noise) if base else spread * noise
        out[name] = jnp.asarray(drawn.astype(out[name].dtype))
    for name, factor in factors.items():
        out[name] = (out[name] * factor).astype(out[name].dtype)
    return out
```

```python
from contextlib import ExitStack
import math

import concourse.bass as bass
from concourse import mybir

F32 = mybir.dt.float32
F32R = mybir.dt.float32r
I32 = mybir.dt.int32
ALU = mybir.AluOpType
ACT = mybir.ActivationFunctionType
AX_X = mybir.AxisListType.X

B, C, N = 32, 128, 1024
HEADS, DH = 8, 64
HID = HEADS * DH
P = 128
NC = N // P
JC = HID // P
HALF = N // 2
OUT, GROUP = 1024, 64
NG = N // GROUP
LN_EPS = 1e-5
NORM_MIN = 1e-12
SLOTS = NC

T_ORDER = [
    [("qT", 6)],
    [("ss", 0), ("qT", 7)],
    [("qT", 0)],
    [("qT", 1)],
    [("ss", 1), ("qT", 2), ("kT", 0), ("kT", 1)],
    [("qT", 3), ("cT", 0), ("cT", 1), ("kT", 2), ("kT", 3)],
    [("qT", 4), ("kT", 4), ("kT", 5)],
    [("qT", 5), ("kT", 6), ("kT", 7), ("xT", 0), ("xT", 1)],
]
PER = {"qT": 8, "ss": 2, "kT": 8, "cT": 2, "xT": 2, "wT": 8}
W_ITERATIONS = (0, 1)


def t_delay(what, n):
    return {"qT": 0 if n < 6 else -1, "ss": -1, "kT": 1, "cT": 1, "xT": -1, "wT": 0}[what]


def t_jobs(t):
    jobs = []
    for i, slot in enumerate(T_ORDER):
        here = list(slot)
        if t in W_ITERATIONS:
            here.append(("wT", i))
        jobs += [(w, n) for w, n in here
                 if t is None or w == "wT" or 0 <= t + t_delay(w, n) < B]
    return jobs


def build(nc, x, ctx_in, wq, wk, wv, wo, bo, g, w_q4, w_scale, f_bias, out):
    x_d = x.rearrange("b c n -> (b c) n")
    c_d = ctx_in.rearrange("b c n -> (b c) n")
    out_d = out.rearrange("b c n -> (b c) n")
    q4_d = w_q4.rearrange("(a p g) j -> a p (g j)", p=P, g=NG)
    scale_d = w_scale.rearrange("(a p g) o -> p a (g o)", p=P, g=NG)

    with ExitStack() as stack:
        def sb(name, shape, dt=F32):
            return stack.enter_context(nc.sbuf_tensor(name, shape, dt))

        def psum(name, shape):
            return stack.enter_context(nc.psum_tensor(name, shape, F32))

        def sem(name):
            return stack.enter_context(nc.semaphore(name))

        ident = sb("ident", [P, P])
        ones_r = sb("ones_r", [P, P], F32R)
        wqT_hi, wqT_lo = sb("wqT_hi", [P, HID], F32R), sb("wqT_lo", [P, HID], F32R)
        wkT_hi, wkT_lo = sb("wkT_hi", [P, HID], F32R), sb("wkT_lo", [P, HID], F32R)
        pT = sb("pT", [P, HEADS * P])
        wT_hi = sb("wT_hi", [P, NC, OUT], F32R)
        wT_lo = sb("wT_lo", [P, NC, OUT], F32R)
        bias_bc = sb("bias_bc", [P, OUT])
        bo_c, g_c = sb("bo_c", [P, 1]), sb("g_c", [P, 1])
        g_neg, bg_neg = sb("g_neg", [P, 1]), sb("bg_neg", [P, 1])
        pow_half, eps_c = sb("pow_half", [P, 1]), sb("eps_c", [P, 1])
        xa = sb("xa", [P, N])
        xn_hi, xn_lo = sb("xn_hi", [P, N], F32R), sb("xn_lo", [P, N], F32R)
        cx = sb("cx", [P, N])
        c_hi, c_lo = sb("c_hi", [P, N], F32R), sb("c_lo", [P, N], F32R)
        cT = sb("cT", [P, NC, P])
        ek = sb("ek", [P, N])
        kT = sb("kT", [P, NC, HID])
        qs = sb("qs", [P, 4, HID])
        qT_hi = sb("qT_hi", [P, 2, JC, HALF], F32R)
        qT_lo = sb("qT_lo", [P, 2, JC, HALF], F32R)
        scratch = sb("scratch", [P, N])
        m_s = scratch[:, 0:HID]
        a_n = scratch[:, HID:2 * HID].rearrange("p (j o) -> p j o", j=JC)
        r0 = scratch
        a_hi, a_lo = sb("a_hi", [P, JC, P], F32R), sb("a_lo", [P, JC, P], F32R)
        sq = sb("sq", [P, HALF])
        sq_hi, sq_lo = sb("sq_hi", [P, HALF], F32R), sb("sq_lo", [P, HALF], F32R)
        o1 = sb("o1", [P, N])
        nrm = sb("nrm", [P, N])
        xr = sb("xr", [P, N])
        x1b = sb("x1b", [P, N])
        xT_hi, xT_lo = sb("xT_hi", [P, NC, P], F32R), sb("xT_lo", [P, NC, P], F32R)
        q_max, q_rz = sb("q_max", [P, 2, HEADS]), sb("q_rz", [P, 4, HEADS])
        k_nmax, k_sum = sb("k_nmax", [P, JC]), sb("k_sum", [P, JC])
        k_sum8, k_rz = sb("k_sum8", [P, JC]), sb("k_rz", [P, JC])
        st1, mv1, ve1, rs1 = sb("st1", [P, 12]), sb("mv1", [P, 2]), sb("ve1", [P, 1]), sb("rs1", [P, 1])
        st2, mv2, ve2, rs2 = sb("st2", [P, 12]), sb("mv2", [P, 2]), sb("ve2", [P, 1]), sb("rs2", [P, 1])

        raw = kT
        q4_i = x1b[:, 0:256].bitcast(I32)
        w_i = x1b[:, 256:768].bitcast(I32)
        w_f = x1b[:, 256:768]
        w_s = x1b[:, 768:896].rearrange("p (a g) -> p a g", g=NG)
        w_s2 = x1b[:, 896:1024].rearrange("p (a g) -> p a g", g=NG)
        ones_f = sq[:, 0:P]

        ql = [psum("ql0", [P, HID]), psum("ql1", [P, HID])]
        tb = [psum("tb0", [P, 512]), psum("tb1", [P, 512])]
        kl = psum("kl", [P, N])
        yb = psum("yb", [P, 512])
        ob = psum("ob", [P, 512])

        x_loaded, ctx_loaded, res_loaded, stored = sem("x_loaded"), sem("ctx_loaded"), sem("res_loaded"), sem("stored")
        raw_loaded, small_loaded, q4_loaded = sem("raw_loaded"), sem("small_loaded"), sem("q4_loaded")
        ones_set, ident_set, raw_turned, raw_copied = sem("ones_set"), sem("ident_set"), sem("raw_turned"), sem("raw_copied")
        woT_copied, p_ready, p_copied, smalls_set, s_gneg = sem("woT_copied"), sem("p_ready"), sem("p_copied"), sem("smalls_set"), sem("s_gneg")
        whi_set, w_bits, w_scaled, w_ready, wT_hi_done = sem("whi_set"), sem("w_bits"), sem("w_scaled"), sem("w_ready"), sem("wT_hi_done")
        q_logits, k_logits, m_ready, a_ready = sem("q_logits"), sem("k_logits"), sem("m_ready"), sem("a_ready")
        out_ready, y_ready = sem("out_ready"), sem("y_ready")
        turned = {w: sem(f"{w}_turned") for w in PER}
        taken = {w: sem(f"{w}_taken") for w in PER}
        q_exp, k_exp, qT_hi_done, xn_hi_done, c_hi_done = sem("q_exp"), sem("k_exp"), sem("qT_hi_done"), sem("xn_hi_done"), sem("c_hi_done")
        m_copied, a_hi_done, sq_done, sq_hi_done, o1_done = sem("m_copied"), sem("a_hi_done"), sem("sq_done"), sem("sq_hi_done"), sem("o1_done")
        norm_done, ln_done, r0_done, xT_hi_done = sem("norm_done"), sem("ln_done"), sem("r0_done"), sem("xT_hi_done")
        q_max_done, q_sub, q_sum_done, q_rz_done, k_max_done = sem("q_max_done"), sem("q_sub"), sem("q_sum_done"), sem("q_rz_done"), sem("k_max_done")
        k_sum8_done, k_rz_done, a_scaled, st1_done, mv1_done = sem("k_sum8_done"), sem("k_rz_done"), sem("a_scaled"), sem("st1_done"), sem("mv1_done")
        xn_done, clamped, r_done, o_scaled = sem("xn_done"), sem("clamped"), sem("r_done"), sem("o_scaled")
        st2_done, mv2_done, xn1_done, result = sem("st2_done"), sem("mv2_done"), sem("xn1_done"), sem("result")
        st_seen = sem("st_seen")
        q_scaled, xn_lo_done, c_lo_done, a_lo_done, sq_lo_done = sem("q_scaled"), sem("xn_lo_done"), sem("c_lo_done"), sem("a_lo_done"), sem("sq_lo_done")
        ve1_done, rs1_done, ve2_done, rs2_done, newton, x1_done, x1b_done = (
            sem("ve1_done"), sem("rs1_done"), sem("ve2_done"), sem("rs2_done"), sem("newton"), sem("x1_done"), sem("x1b_done"))

        def wait(eng, semaphore, per, t, delay, n):
            if isinstance(t, int) and t + delay >= B:
                return
            until(eng, semaphore, t * per + (delay * per + n))

        def until(eng, semaphore, value):
            if not isinstance(value, int) or value > 0:
                eng.wait_ge(semaphore, value)

        def live(t, delay):
            return not isinstance(t, int) or 0 <= t + delay < B

        def pipeline(eng, iteration, first):
            for t in range(first, 3):
                iteration(t)
            with eng.Fori(3, B - 2) as t:
                iteration(t)
            for t in range(B - 2, B + 2):
                iteration(t)

        def three_passes(pe, dst, w_hi, w_lo, m_hi, m_lo, start, stop):
            pe.matmul(dst, w_hi, m_hi, start=start, stop=False)
            pe.matmul(dst, w_hi, m_lo, start=False, stop=False)
            return pe.matmul(dst, w_lo, m_hi, start=False, stop=stop)

        block = stack.enter_context(nc.Block())

        @block.sync
        def _(sp):
            sp.dma_start(raw[:, 0, :].rearrange("p (j c) -> p j c", j=JC),
                         wq.rearrange("(j p) c -> p j c", p=P)).then_inc(raw_loaded, 16)
            sp.dma_start(raw[:, 1, :].rearrange("p (j c) -> p j c", j=JC),
                         wk.rearrange("(j p) c -> p j c", p=P)).then_inc(raw_loaded, 16)
            sp.dma_start(raw[:, 2, :].rearrange("p (j c) -> p j c", j=JC),
                         wv.rearrange("(j p) c -> p j c", p=P)).then_inc(raw_loaded, 16)
            sp.dma_start(raw[:, 3, :], wo).then_inc(raw_loaded, 16)
            sp.dma_start(bo_c[:], bo.rearrange("(c o) -> c o", o=1)).then_inc(small_loaded, 16)
            sp.dma_start(g_c[:], g.rearrange("a c o -> (a c) o")).then_inc(small_loaded, 16)
            sp.dma_start(w_s, scale_d).then_inc(small_loaded, 16)
            sp.dma_start(bias_bc[:], f_bias.rearrange("(a n) -> a n", a=1).to_broadcast([P, OUT])).then_inc(small_loaded, 16)

            def iteration(t):
                def value(v):
                    return v if isinstance(v, int) else sp.snap(v)

                row = {d: value((t + d) * P) for d in (1, -1, 2, -2) if live(t, d)}
                x_free, x1_used, c_turned, done = (value(v) for v in (2 * t + 2, t - 1, 2 * t + 4, 2 * t - 2))
                if live(t, 1):
                    until(sp, xn_lo_done, x_free)
                    sp.dma_start(xa[:], x_d[bass.ds(row[1], P), :]).then_inc(x_loaded, 16)
                if live(t, -1):
                    until(sp, x1b_done, x1_used)
                    until(sp, xn1_done, x1_used)
                    sp.dma_start(xr[:], x_d[bass.ds(row[-1], P), :]).then_inc(res_loaded, 16)
                if live(t, 2):
                    until(sp, turned["cT"], c_turned)
                    sp.dma_start(cx[:], c_d[bass.ds(row[2], P), :]).then_inc(ctx_loaded, 16)
                if live(t, -2):
                    until(sp, result, done)
                    sp.dma_start(out_d[bass.ds(row[-2], P), :], x1b[:]).then_inc(stored, 16)

            for t in (-2, -1, 0, 1, 2):
                iteration(t)
            with sp.Fori(3, B - 2) as t:
                iteration(t)
            for t in range(B - 2, B + 2):
                iteration(t)
            sp.wait_ge(stored, 16 * B)

        @block.tensor
        def _(pe):
            pe.wait_ge(ident_set, 1)
            pe.wait_ge(raw_loaded, 64)
            for which, bank in ((0, ql[0]), (1, ql[1]), (3, ob)):
                for j in range(JC):
                    mm = pe.transpose(bank[:, j * P:(j + 1) * P], raw[:, which, j * P:(j + 1) * P], ident[:])
                mm.then_inc(raw_turned, 1)
            pe.wait_ge(woT_copied, 1)
            for h in range(HEADS):
                r = slice(DH * (h % 2), DH * (h % 2) + DH)
                j = slice((h // 2) * P, (h // 2 + 1) * P)
                at = HALF * (h % 2) + P * (h // 2)
                mm = pe.matmul(kl[:, at:at + P], raw[r, 2, j], raw[r, 4, j], start=True, stop=True)
            mm.then_inc(p_ready, 1)
            pe.wait_ge(raw_copied, 2)
            pe.wait_ge(p_copied, 1)

            def iteration(t):
                jobs = t_jobs(t if isinstance(t, int) else None)
                before = []
                if isinstance(t, int):
                    for s in range(-1, t):
                        before += [(s - t, w, n) for w, n in t_jobs(s)]
                else:
                    before = [(-1, w, n) for w, n in t_jobs(None)]
                line = before + [(0, w, n) for w, n in jobs]

                def bank_for(what, n):
                    at = line.index((0, what, n))
                    if at >= 2:
                        back, w, m = line[at - 2]
                        if w == "wT":
                            pe.wait_ge(taken[w], SLOTS * (t + back) + m + 1)
                        else:
                            wait(pe, taken[w], PER[w], t, back + t_delay(w, m), m + 1)
                    return tb[at % 2]

                def turn_q(i, delay):
                    wait(pe, q_scaled, 8, t, delay, i + 1)
                    bank = bank_for("qT", i)
                    for j in range(JC):
                        mm = pe.transpose(bank[:, j * P:(j + 1) * P], qs[:, i % 4, j * P:(j + 1) * P], ident[:])
                    mm.then_inc(turned["qT"], 1)

                def turn_k(j):
                    wait(pe, k_exp, 4, t, 1, j + 1)
                    for half in range(2):
                        bank = bank_for("kT", 2 * j + half)
                        for c in range(4):
                            n = 4 * half + c
                            mm = pe.transpose(bank[:, c * P:(c + 1) * P], ek[:, n * P:(n + 1) * P], ident[:])
                        mm.then_inc(turned["kT"], 1)

                def turn_rows(what, src):
                    for half in range(2):
                        bank = bank_for(what, half)
                        for c in range(4):
                            n = 4 * half + c
                            mm = pe.transpose(bank[:, c * P:(c + 1) * P], src[:, n * P:(n + 1) * P], ident[:])
                        mm.then_inc(turned[what], 1)

                def k_logit(j):
                    if j == 0:
                        wait(pe, c_lo_done, 1, t, 1, 1)
                        wait(pe, a_scaled, 2, t, 0, 2)
                    wait(pe, k_exp, 4, t, 1, j)
                    w = slice(j * P, (j + 1) * P)
                    for half in range(2):
                        m = slice(half * HALF, (half + 1) * HALF)
                        mm = three_passes(pe, kl[:, m], wkT_hi[:, w], wkT_lo[:, w], c_hi[:, m], c_lo[:, m], True, True)
                    mm.then_inc(k_logits, 1)

                def ffn(p):
                    half = p // 4
                    if p == 0:
                        wait(pe, taken["xT"], 2, t, -2, 2)
                        wait(pe, result, 2, t, -3, 2)
                        if isinstance(t, int) and t == 2:
                            pe.wait_ge(taken["wT"], 16)
                    if p == 4:
                        wait(pe, result, 2, t, -2, 1)
                    o = slice(half * HALF, (half + 1) * HALF)
                    for c in (2 * (p % 4), 2 * (p % 4) + 1):
                        mm = three_passes(pe, yb[:], xT_hi[:, c, :], xT_lo[:, c, :],
                                          wT_hi[:, c, o], wT_lo[:, c, o], c == 0, c == NC - 1)
                    if p % 4 == 3:
                        mm.then_inc(y_ready, 1)

                def m_part(p):
                    if p == 0:
                        wait(pe, taken["kT"], 8, t, 0, 8)
                        wait(pe, taken["cT"], 2, t, 0, 2)
                        wait(pe, o1_done, 2, t, -1, 1)
                    for c in (2 * p, 2 * p + 1):
                        mm = pe.matmul(ob[:], cT[:, c, :], kT[:, c, :], start=(c == 0), stop=(c == NC - 1))
                    if p == 3:
                        mm.then_inc(m_ready, 1)

                def a_part():
                    wait(pe, m_copied, 1, t, 0, 1)
                    wait(pe, k_exp, 4, t, 0, 4)
                    for j in range(JC):
                        mm = pe.matmul(kl[:, j * 2 * P:(j + 1) * 2 * P], m_s[:, j * P:(j + 1) * P],
                                       pT[:, j * 2 * P:(j + 1) * 2 * P], start=True, stop=True)
                    mm.then_inc(a_ready, 1)

                def out_half(half, delay):
                    if half == 0:
                        wait(pe, taken["qT"], 8, t, delay, 4)
                        wait(pe, a_lo_done, 1, t, delay, 1)
                        wait(pe, o1_done, 2, t, -1, 2)
                    else:
                        wait(pe, taken["qT"], 8, t, delay, 8)
                        wait(pe, m_copied, 1, t, 0, 1)
                    for j in range(JC):
                        mm = three_passes(pe, ob[:], a_hi[:, j, :], a_lo[:, j, :],
                                          qT_hi[:, half, j, :], qT_lo[:, half, j, :], j == 0, j == JC - 1)
                    mm.then_inc(out_ready, 1)

                def squares(half):
                    wait(pe, sq_lo_done, 2, t, -1, half + 1)
                    bank = bank_for("ss", half)
                    pe.matmul(bank[:], ones_r[:], sq_hi[:], start=True, stop=False)
                    pe.matmul(bank[:], ones_r[:], sq_lo[:], start=False, stop=True).then_inc(turned["ss"], 1)

                for i in range(SLOTS):
                    q, q_old, keys, tail, feed = live(t, 0), live(t, -1), live(t, 1), live(t, -1), live(t, -2)
                    if q:
                        if i % 4 == 0:
                            wait(pe, xn_lo_done, 2, t, 0, 1 + i // 4)
                        wait(pe, q_sub, 8, t, 0, i - 1)
                        r = slice(i * P, (i + 1) * P)
                        three_passes(pe, ql[i % 2][:], xn_hi[:, r], xn_lo[:, r], wqT_hi[:], wqT_lo[:],
                                     True, True).then_inc(q_logits, 1)
                    if i == 1 and tail:
                        squares(0)
                    if i == 4 and tail:
                        squares(1)
                    if i < 2 and q_old:
                        turn_q(i + 6, -1)
                    if i >= 2 and q:
                        turn_q(i - 2, 0)
                    if i == 0:
                        if feed:
                            ffn(0)
                        if q:
                            m_part(0)
                            m_part(1)
                    if i == 1:
                        if q:
                            m_part(2)
                            m_part(3)
                        if feed:
                            ffn(1)
                    if i == 2:
                        if q_old:
                            if not q:
                                pass
                            out_half(1, -1)
                        if feed:
                            ffn(2)
                        if q:
                            a_part()
                    if i == 3:
                        if feed:
                            ffn(3)
                        if keys:
                            k_logit(0)
                        if feed:
                            ffn(4)
                    if i == 5 and keys:
                        wait(pe, ctx_loaded, 16, t, 1, 16)
                        if t is None:
                            pass
                        turn_rows("cT", cx)
                    if 4 <= i <= 6:
                        if feed:
                            ffn(i + 1)
                        if keys:
                            turn_k(i - 4)
                            k_logit(i - 3)
                    if i == 7:
                        if keys:
                            turn_k(3)
                        if tail:
                            wait(pe, xn1_done, 1, t, -1, 1)
                            turn_rows("xT", nrm)
                        if q:
                            out_half(0, 0)
                    if isinstance(t, int) and t in W_ITERATIONS:
                        pe.wait_ge(w_ready, SLOTS * t + i + 1)
                        bank = bank_for("wT", i)
                        for c in range(4):
                            mm = pe.transpose(bank[:, c * P:(c + 1) * P], w_f[:, c * P:(c + 1) * P], ident[:])
                        mm.then_inc(turned["wT"], 1)

            pipeline(pe, iteration, -1)

        def bank_of(t, what, n):
            if isinstance(t, int):
                at = sum(len(t_jobs(s)) for s in range(-1, t)) + t_jobs(t).index((what, n))
            else:
                at = sum(len(t_jobs(s)) for s in range(-1, 3)) + t_jobs(None).index((what, n))
            return tb[at % 2]

        @block.scalar
        def _(act):
            nc.scalar.preload_act_table_set("natural_log_exp_and_others")
            act.wait_ge(raw_turned, 1)
            nc.scalar.copy(wqT_hi[:], ql[0][:]).then_inc(whi_set, 1)
            act.wait_ge(raw_turned, 2)
            nc.scalar.copy(wkT_hi[:], ql[1][:]).then_inc(whi_set, 1)
            act.wait_ge(raw_turned, 3)
            nc.scalar.copy(raw[:, 4, :], ob[:]).then_inc(woT_copied, 1)
            act.wait_ge(p_ready, 1)
            nc.scalar.copy(pT[:].rearrange("p (j a o) -> p a j o", j=JC, a=2),
                           kl[:].rearrange("p (a j o) -> p a j o", j=JC, a=2)).then_inc(p_copied, 1)
            act.wait_ge(smalls_set, 3)

            def iteration(t):
                q, q_old, keys, tail, feed = live(t, 0), live(t, -1), live(t, 1), live(t, -1), live(t, -2)

                def split_q(i, delay):
                    wait(act, turned["qT"], 8, t, delay, i + 1)
                    if i % 4 == 0:
                        wait(act, out_ready, 2, t, delay - 1, i // 4 + 1)
                    nc.scalar.copy(qT_hi[:, i // 4, :, (i % 4) * P:(i % 4 + 1) * P],
                                   bank_of(t, "qT", i)[:].rearrange("p (j n) -> p j n", j=JC)).then_inc(qT_hi_done, 1)

                def q_exponent(i):
                    wait(act, q_sub, 8, t, 0, i + 1)
                    nc.scalar.activation(qs[:, i % 4, :], qs[:, i % 4, :], ACT.Exp).then_inc(q_exp, 1)

                def k_exponent(j):
                    wait(act, k_max_done, 4, t, 1, j + 1)
                    wait(act, turned["kT"], 8, t, 1, 2 * j)
                    if j == 0:
                        wait(act, k_sum8_done, 1, t, 0, 1)
                    nc.scalar.activation(ek[:], kl[:], ACT.Exp, bias=k_nmax[:, j:j + 1],
                                         accum_out=k_sum[:, j:j + 1]).then_inc(k_exp, 1)

                def copy_k(j):
                    for half in range(2):
                        wait(act, turned["kT"], 8, t, 1, 2 * j + half + 1)
                        if j == 0 and half == 0:
                            wait(act, m_ready, 1, t, 0, 1)
                        nc.scalar.copy(kT[:, 4 * half:4 * half + 4, j * P:(j + 1) * P],
                                       bank_of(t, "kT", 2 * j + half)[:].rearrange("p (c k) -> p c k", c=4)
                                       ).then_inc(taken["kT"], 1)

                def leave_out(half):
                    wait(act, out_ready, 2, t, -1, half + 1)
                    wait(act, sq_lo_done, 2, t, -1, half)
                    nc.scalar.activation(sq[:], ob[:], ACT.Square, bias=bo_c[:]).then_inc(sq_done, 1)
                    wait(act, turned["ss"], 2, t, -1, half)
                    nc.scalar.activation(sq_hi[:], ob[:], ACT.Square, bias=bo_c[:]).then_inc(sq_hi_done, 1)
                    if half == 0:
                        wait(act, x1_done, 1, t, -2, 1)
                    nc.scalar.activation(o1[:, half * HALF:(half + 1) * HALF], ob[:], ACT.Identity,
                                         bias=bg_neg[:], scale=g_neg[:]).then_inc(o1_done, 1)

                def copy_squares(half):
                    wait(act, turned["ss"], 2, t, -1, half + 1)
                    if half == 0:
                        wait(act, turned["xT"], 2, t, -2, 2)
                    nc.scalar.copy(nrm[:, half * HALF:(half + 1) * HALF],
                                   bank_of(t, "ss", half)[:]).then_inc(taken["ss"], 1)

                def split_xn(half, delay):
                    h = slice(half * HALF, (half + 1) * HALF)
                    wait(act, xn_done, 2, t, delay, half + 1)
                    wait(act, q_logits, 8, t, delay - 1, 4 * half + 4)
                    nc.scalar.copy(xn_hi[:, h], xa[:, h]).then_inc(xn_hi_done, 1)

                for i in range(SLOTS):
                    if i in (0, 3) and tail:
                        leave_out(0 if i == 0 else 1)
                    if i >= 4 and keys:
                        k_exponent(i - 4)
                    if i == 1 and tail:
                        copy_squares(0)
                    if i == 4 and tail:
                        copy_squares(1)
                    if i == 2 and q:
                        wait(act, m_ready, 1, t, 0, 1)
                        wait(act, o_scaled, 1, t, -2, 1)
                        nc.scalar.copy(m_s[:], ob[:]).then_inc(m_copied, 1)
                    if i < 2 and q_old:
                        split_q(i + 6, -1)
                    if i >= 2 and q:
                        split_q(i - 2, 0)
                    if i == 4 and tail:
                        wait(act, taken["ss"], 2, t, -1, 2)
                        nc.scalar.activation(nrm[:], nrm[:], ACT.Sqrt).then_inc(norm_done, 1)
                        nc.scalar.preload_act_table_set("natural_log_exp_and_others")
                    if i == 3 and q:
                        wait(act, a_scaled, 2, t, 0, 2)
                        wait(act, out_ready, 2, t, -1, 2)
                        nc.scalar.copy(a_hi[:], a_n[:]).then_inc(a_hi_done, 1)
                    if i == 5 and keys:
                        for half in range(2):
                            wait(act, turned["cT"], 2, t, 1, half + 1)
                            if half == 0:
                                wait(act, m_ready, 1, t, 0, 1)
                            nc.scalar.copy(cT[:, 4 * half:4 * half + 4, :],
                                           bank_of(t, "cT", half)[:].rearrange("p (c k) -> p c k", c=4)
                                           ).then_inc(taken["cT"], 1)
                    if i >= 4 and keys:
                        copy_k(i - 4)
                    if i == 4 and tail:
                        wait(act, clamped, 1, t, -1, 1)
                        wait(act, a_ready, 1, t, 0, 1) if q else None
                        wait(act, a_lo_done, 1, t, 0, 1) if q else None
                        nc.scalar.activation(r0[:], nrm[:], ACT.Ln).then_inc(ln_done, 1)
                        wait(act, ln_done, 1, t, -1, 1)
                        nc.scalar.activation(r0[:], r0[:], ACT.Exp, scale=-1.0).then_inc(r0_done, 1)
                    if q:
                        q_exponent(i)
                    if i == 0 and q:
                        split_xn(1, 0)
                    if i == 5 and keys:
                        split_xn(0, 1)
                    if i == 1 and keys:
                        wait(act, ctx_loaded, 16, t, 1, 16)
                        wait(act, k_logits, 4, t, 0, 4)
                        nc.scalar.copy(c_hi[:], cx[:]).then_inc(c_hi_done, 1)
                    if i == 7 and tail:
                        for half in range(2):
                            wait(act, turned["xT"], 2, t, -1, half + 1)
                            if half == 0:
                                wait(act, y_ready, 2, t, -2, 2)
                            nc.scalar.copy(xT_hi[:, 4 * half:4 * half + 4, :],
                                           bank_of(t, "xT", half)[:].rearrange("p (c k) -> p c k", c=4)
                                           ).then_inc(xT_hi_done, 1)
                    if isinstance(t, int) and t in W_ITERATIONS:
                        u = SLOTS * t + i
                        act.wait_ge(turned["wT"], u + 1)
                        a, wh = u // 2, u % 2
                        nc.scalar.copy(wT_hi[:, 4 * wh:4 * wh + 4, a * P:(a + 1) * P],
                                       bank_of(t, "wT", i)[:].rearrange("p (c k) -> p c k", c=4)).then_inc(wT_hi_done, 1)
                    if isinstance(t, int) and 0 <= SLOTS * t + i + 1 < 2 * OUT // P:
                        u = SLOTS * t + i + 1
                        until(act, w_bits, 2 * u)
                        act.dma_start(q4_i, q4_d[u // 2, :, 256 * (u % 2):256 * (u % 2) + 256]).then_inc(q4_loaded, 16)

            pipeline(act, iteration, -1)

        @block.vector
        def _(dve):
            nc.vector.memset(ones_f, 1.0).then_inc(ones_set, 1)
            nc.vector.memset(pow_half[:], -0.5).then_inc(ones_set, 1)
            nc.vector.memset(eps_c[:], LN_EPS).then_inc(ones_set, 1)
            dve.wait_ge(ones_set, 3)
            nc.vector.tensor_copy(ones_r[:], ones_f).then_inc(smalls_set, 1)
            dve.wait_ge(small_loaded, 64)
            nc.vector.tensor_scalar(g_neg[:], g_c[:], -math.sqrt(C), None, ALU.mult).then_inc(s_gneg, 1)
            nc.vector.tensor_scalar(w_s2, w_s, 2.0 / 15.0, None, ALU.mult).then_inc(smalls_set, 1)
            dve.wait_ge(s_gneg, 1)
            nc.vector.tensor_tensor(bg_neg[:], bo_c[:], g_neg[:], ALU.mult).then_inc(smalls_set, 1)
            dve.wait_ge(whi_set, 1)
            nc.vector.tensor_tensor(wqT_lo[:], ql[0][:], wqT_hi[:], ALU.subtract).then_inc(raw_copied, 1)
            dve.wait_ge(whi_set, 2)
            nc.vector.tensor_tensor(wkT_lo[:], ql[1][:], wkT_hi[:], ALU.subtract).then_inc(raw_copied, 1)
            dve.wait_ge(smalls_set, 3)

            def heads(ap):
                return ap.rearrange("p (h d) -> p h d", h=HEADS)

            def iteration(t):
                q, q_old, keys, tail, feed = live(t, 0), live(t, -1), live(t, 1), live(t, -1), live(t, -2)

                def q_maximum(i):
                    wait(dve, q_logits, 8, t, 0, i + 1)
                    nc.vector.tensor_reduce(q_max[:, i % 2, :], heads(ql[i % 2][:]), AX_X, ALU.max).then_inc(q_max_done, 1)

                def q_subtract(i):
                    wait(dve, q_max_done, 8, t, 0, i + 1)
                    wait(dve, turned["qT"], 8, t, 0, i - 3)
                    nc.vector.tensor_tensor(heads(qs[:, i % 4, :]), heads(ql[i % 2][:]),
                                            q_max[:, i % 2, :].unsqueeze(2).to_broadcast([P, HEADS, DH]),
                                            ALU.subtract).then_inc(q_sub, 1)

                def q_total(i, delay):
                    wait(dve, q_exp, 8, t, delay, i + 1)
                    nc.vector.tensor_reduce(q_rz[:, i % 4, :], heads(qs[:, i % 4, :]), AX_X, ALU.add).then_inc(q_sum_done, 1)

                def q_reciprocal(i, delay):
                    wait(dve, q_sum_done, 8, t, delay, i + 1)
                    nc.vector.reciprocal(q_rz[:, i % 4, :], q_rz[:, i % 4, :]).then_inc(q_rz_done, 1)

                def lo_q(i, delay):
                    at = (slice(None), i // 4, slice(None), slice((i % 4) * P, (i % 4 + 1) * P))
                    wait(dve, qT_hi_done, 8, t, delay, i + 1)
                    nc.vector.tensor_tensor(qT_lo[at], bank_of(t, "qT", i)[:].rearrange("p (j n) -> p j n", j=JC),
                                            qT_hi[at], ALU.subtract).then_inc(taken["qT"], 1)

                def k_maximum(j):
                    wait(dve, k_logits, 4, t, 1, j + 1)
                    nc.vector.tensor_reduce(k_nmax[:, j:j + 1], kl[:], AX_X, ALU.max, negate=True).then_inc(k_max_done, 1)

                def normalise_x(half, delay):
                    h = slice(half * HALF, (half + 1) * HALF)
                    wait(dve, rs1_done, 1, t, delay, 1)
                    nc.vector.tensor_scalar(xa[:, h], xa[:, h], mv1[:, 0:1], rs1[:], ALU.subtract, ALU.mult
                                            ).then_inc(xn_done, 1)

                def finish(half):
                    h = slice(half * HALF, (half + 1) * HALF)
                    wait(dve, y_ready, 2, t, -2, half + 1)
                    if half == 0:
                        wait(dve, x1b_done, 1, t, -2, 1)
                    nc.vector.tensor_tensor(x1b[:, h], yb[:], x1b[:, h], ALU.add).then_inc(result, 1)

                for i in range(SLOTS):
                    if isinstance(t, int) and t in W_ITERATIONS:
                        u = SLOTS * t + i
                        a, wh = u // 2, u % 2
                        pairs = w_i.rearrange("p (n two) -> p n two", two=2)
                        dve.wait_ge(q4_loaded, 16 * (u + 1))
                        wait(dve, turned["wT"], 1, u, 0, 0)
                        nc.vector.tensor_scalar(pairs[:, :, 0], q4_i, 15, None, ALU.bitwise_and).then_inc(w_bits, 1)
                        nc.vector.tensor_scalar(pairs[:, :, 1], q4_i, 4, 15, ALU.logical_shift_right,
                                                ALU.bitwise_and).then_inc(w_bits, 1)
                    if q:
                        q_maximum(i)
                    if i == 0 and q_old:
                        q_total(7, -1)
                    if i > 0 and q:
                        q_total(i - 1, 0)
                    if isinstance(t, int) and t in W_ITERATIONS:
                        dve.wait_ge(w_bits, 2 * (u + 1))
                        nc.vector.tensor_tensor(
                            w_f.rearrange("p (g e) -> p g e", e=GROUP), w_i.rearrange("p (g e) -> p g e", e=GROUP),
                            w_s2[:, a, 8 * wh:8 * wh + 8].unsqueeze(2).to_broadcast([P, 8, GROUP]),
                            ALU.mult).then_inc(w_scaled, 1)
                    if i == 0 and q:
                        wait(dve, k_exp, 4, t, 0, 4)
                        nc.vector.tensor_scalar(k_sum8[:], k_sum[:], math.sqrt(DH), None, ALU.mult).then_inc(k_sum8_done, 1)
                    if q:
                        q_subtract(i)
                    if i == 0 and q_old:
                        q_reciprocal(7, -1)
                    if i > 0 and q:
                        q_reciprocal(i - 1, 0)
                    if i == 0 and q:
                        wait(dve, k_sum8_done, 1, t, 0, 1)
                        nc.vector.reciprocal(k_rz[:], k_sum8[:]).then_inc(k_rz_done, 1)
                        normalise_x(1, 0)
                    if i == 2 and keys:
                        wait(dve, x_loaded, 16, t, 1, 16)
                        for half in range(2):
                            nc.vector.bn_stats(st1[:, 6 * half:6 * half + 6], xa[:, half * HALF:(half + 1) * HALF]).then_inc(st1_done, 1)
                    if i == 3 and q:
                        wait(dve, a_ready, 1, t, 0, 1)
                        wait(dve, k_rz_done, 1, t, 0, 1)
                        for head in range(2):
                            r = slice(DH * head, DH * (head + 1))
                            nc.vector.tensor_tensor(
                                a_n[r], kl[r].rearrange("p (j a o) -> p j a o", j=JC, a=2)[:, :, head, :],
                                k_rz[r, :].unsqueeze(2).to_broadcast([DH, JC, P]), ALU.mult).then_inc(a_scaled, 1)
                    if i < 2 and q_old:
                        lo_q(i + 6, -1)
                    if i >= 2 and q:
                        lo_q(i - 2, 0)
                    if i == 2 and keys:
                        wait(dve, st1_done, 2, t, 1, 2)
                        dve.sem_inc(st_seen, 1)
                        nc.vector.bn_aggr(mv1[:], st1[:]).then_inc(mv1_done, 1)
                    if i == 4 and tail:
                        wait(dve, norm_done, 1, t, -1, 1)
                        nc.vector.tensor_scalar(nrm[:], nrm[:], NORM_MIN, None, ALU.max).then_inc(clamped, 1)
                    if i == 3 and feed:
                        finish(0)
                    if i == 4 and keys:
                        normalise_x(0, 1)
                    if i == 5 and tail:
                        wait(dve, newton, 1, t, -1, 1)
                        nc.vector.scalar_tensor_tensor(out=nrm[:], in0=nrm[:], scalar=-2.0, in1=r0[:],
                                                       op0=ALU.add, op1=ALU.mult).then_inc(r_done, 1)
                    if 3 <= i <= 6 and keys:
                        k_maximum(i - 3)
                    if i == 5 and tail:
                        wait(dve, r_done, 1, t, -1, 1)
                        wait(dve, o1_done, 2, t, -1, 2)
                        nc.vector.tensor_tensor(o1[:], o1[:], nrm[:], ALU.mult).then_inc(o_scaled, 1)
                    if i == 6 and tail:
                        wait(dve, x1_done, 1, t, -1, 1)
                        for half in range(2):
                            nc.vector.bn_stats(st2[:, 6 * half:6 * half + 6], xr[:, half * HALF:(half + 1) * HALF]).then_inc(st2_done, 1)
                        wait(dve, st2_done, 2, t, -1, 2)
                        dve.sem_inc(st_seen, 1)
                        nc.vector.bn_aggr(mv2[:], st2[:]).then_inc(mv2_done, 1)
                    if i == 7 and tail:
                        wait(dve, rs2_done, 1, t, -1, 1)
                        nc.vector.tensor_scalar(nrm[:], xr[:], mv2[:, 0:1], rs2[:], ALU.subtract, ALU.mult
                                                ).then_inc(xn1_done, 1)
                    if i == 7 and feed:
                        finish(1)
                    if i == 7 and tail:
                        for half in range(2):
                            at = slice(4 * half, 4 * half + 4)
                            wait(dve, xT_hi_done, 2, t, -1, half + 1)
                            nc.vector.tensor_tensor(xT_lo[:, at, :], bank_of(t, "xT", half)[:].rearrange("p (c k) -> p c k", c=4),
                                                    xT_hi[:, at, :], ALU.subtract).then_inc(taken["xT"], 1)
                    if isinstance(t, int) and t in W_ITERATIONS:
                        at = (slice(None), slice(4 * wh, 4 * wh + 4), slice(a * P, (a + 1) * P))
                        dve.wait_ge(wT_hi_done, u + 1)
                        nc.vector.tensor_tensor(wT_lo[at], bank_of(t, "wT", i)[:].rearrange("p (c k) -> p c k", c=4),
                                                wT_hi[at], ALU.subtract).then_inc(taken["wT"], 1)

            pipeline(dve, iteration, -1)

        @block.gpsimd
        def _(pool):
            pool.wait_ge(ones_set, 3)
            nc.gpsimd.affine_select(out=ident[:], in_=ones_f, compare_op=ALU.is_equal, fill=0.0, base=0,
                                    pattern=[[-1, P]], channel_multiplier=1).then_inc(ident_set, 1)
            pool.wait_ge(small_loaded, 64)

            def iteration(t):
                q, q_old, keys, tail, feed = live(t, 0), live(t, -1), live(t, 1), live(t, -1), live(t, -2)

                def scale_q(i, delay):
                    wait(pool, q_rz_done, 8, t, delay, i + 1)
                    v = qs[:, i % 4, :].rearrange("p (h d) -> p h d", h=HEADS)
                    nc.gpsimd.tensor_tensor(v, v, q_rz[:, i % 4, :].unsqueeze(2).to_broadcast([P, HEADS, DH]),
                                            ALU.mult).then_inc(q_scaled, 1)

                def lo_xn(half, delay):
                    h = slice(half * HALF, (half + 1) * HALF)
                    wait(pool, xn_hi_done, 2, t, delay, half + 1)
                    nc.gpsimd.tensor_tensor(xn_lo[:, h], xa[:, h], xn_hi[:, h], ALU.subtract).then_inc(xn_lo_done, 1)

                def lo_squares(half):
                    wait(pool, sq_hi_done, 2, t, -1, half + 1)
                    nc.gpsimd.tensor_tensor(sq_lo[:], sq[:], sq_hi[:], ALU.subtract).then_inc(sq_lo_done, 1)

                def deviation(delay, mv_done, mv, ve_done, ve, rs_done, rs):
                    wait(pool, mv_done, 1, t, delay, 1)
                    nc.gpsimd.tensor_tensor(ve[:], mv[:, 1:2], eps_c[:], ALU.add).then_inc(ve_done, 1)
                    wait(pool, ve_done, 1, t, delay, 1)
                    nc.gpsimd.tensor_tensor(rs[:], ve[:], pow_half[:], ALU.pow).then_inc(rs_done, 1)

                for i in range(SLOTS):
                    if i == 7 and tail:
                        deviation(-1, mv2_done, mv2, ve2_done, ve2, rs2_done, rs2)
                    if i == 0 and q_old:
                        scale_q(7, -1)
                    if i > 0 and q:
                        scale_q(i - 1, 0)
                    if i in (0, 3) and tail:
                        lo_squares(0 if i == 0 else 1)
                    if i == 0 and q:
                        lo_xn(1, 0)
                    if i == 1 and keys:
                        wait(pool, c_hi_done, 1, t, 1, 1)
                        nc.gpsimd.tensor_tensor(c_lo[:], cx[:], c_hi[:], ALU.subtract).then_inc(c_lo_done, 1)
                    if i == 1 and feed:
                        wait(pool, stored, 16, t, -3, 16)
                        if isinstance(t, int) and t == 2:
                            pool.wait_ge(turned["wT"], 16)
                        nc.gpsimd.tensor_tensor(x1b[:], xr[:], bias_bc[:], ALU.add).then_inc(x1b_done, 1)
                    if i == 2 and keys:
                        deviation(1, mv1_done, mv1, ve1_done, ve1, rs1_done, rs1)
                    if i == 3 and q:
                        wait(pool, a_hi_done, 1, t, 0, 1)
                        nc.gpsimd.tensor_tensor(a_lo[:], a_n[:], a_hi[:], ALU.subtract).then_inc(a_lo_done, 1)
                    if i == 4 and tail:
                        wait(pool, r0_done, 1, t, -1, 1)
                        nc.gpsimd.tensor_tensor(nrm[:], nrm[:], r0[:], ALU.mult).then_inc(newton, 1)
                    if i == 5 and keys:
                        lo_xn(0, 1)
                    if i == 6 and tail:
                        wait(pool, o_scaled, 1, t, -1, 1)
                        wait(pool, res_loaded, 16, t, -1, 16)
                        nc.gpsimd.tensor_tensor(xr[:], o1[:], xr[:], ALU.add).then_inc(x1_done, 1)
                    if isinstance(t, int) and t in W_ITERATIONS:
                        u = SLOTS * t + i
                        a, wh = u // 2, u % 2
                        pool.wait_ge(w_scaled, u + 1)
                        v = w_f.rearrange("p (g e) -> p g e", e=GROUP)
                        nc.gpsimd.tensor_tensor(v, v, w_s[:, a, 8 * wh:8 * wh + 8].unsqueeze(2).to_broadcast([P, 8, GROUP]),
                                                ALU.subtract).then_inc(w_ready, 1)

            pipeline(pool, iteration, -1)


_INS = ["x", "ctx_4096", "L0_xattn_Wq", "L0_xattn_Wk", "L0_xattn_Wv", "L0_xattn_Wo", "L0_xattn_bo", "L0_xattn_g",
        "L0_ffn_weight_q4", "L0_ffn_weight_scale", "L0_ffn_bias"]


def kernel(**inputs):
    import numpy as _np
    import concourse.bacc as _bacc
    from concourse import mybir as _mybir
    from concourse.bass_utils import run_bass_kernel_spmd as _run

    nc = _bacc.Bacc("TRN2", target_bir_lowering=False, num_devices=1)
    arrays, args = {}, []
    for name in _INS:
        a = _np.ascontiguousarray(inputs[name])
        arrays[f"in_{name}_dram"] = a
        args.append(nc.dram_tensor(f"in_{name}_dram", a.shape, _mybir.dt.from_np(a.dtype), kind="ExternalInput").ap())
    args.append(nc.dram_tensor("out_0_dram", (B, C, N), _mybir.dt.float32, kind="ExternalOutput").ap())
    build(nc, *args)
    r = _run(nc, [arrays], core_ids=[0])
    return r.results[0]["out_0_dram"]
```

```python
from contextlib import ExitStack
import math

import concourse.bass as bass
from concourse import mybir

F32 = mybir.dt.float32
F32R = mybir.dt.float32r
I32 = mybir.dt.int32
ALU = mybir.AluOpType
ACT = mybir.ActivationFunctionType
AX_X = mybir.AxisListType.X

B, C, N = 32, 128, 1024
HEADS, DH = 8, 64
HID = HEADS * DH
P = 128
NC = N // P
JC = HID // P
HALF = N // 2
OUT, GROUP = 1024, 64
NG = N // GROUP
LN_EPS = 1e-5
NORM_MIN = 1e-12
SLOTS = NC

T_ORDER = [
    [("qT", 6), ("xT", 0), ("xT", 1)],
    [("ss", 0), ("qT", 7)],
    [("qT", 0)],
    [("ss", 1), ("qT", 1)],
    [("qT", 2), ("kT", 0), ("kT", 1)],
    [("qT", 3), ("cT", 0), ("kT", 2), ("kT", 3)],
    [("qT", 4), ("cT", 1), ("kT", 4), ("kT", 5)],
    [("qT", 5), ("kT", 6), ("kT", 7)],
]
PER = {"qT": 8, "ss": 2, "kT": 8, "cT": 2, "xT": 2, "wT": 8}
W_ITERATIONS = (0, 1)


def t_delay(what, n):
    return {"qT": 0 if n < 6 else -1, "ss": -1, "kT": 1, "cT": 1, "xT": -2, "wT": 0}[what]


def t_jobs(t):
    jobs = []
    for i, slot in enumerate(T_ORDER):
        here = list(slot)
        if t in W_ITERATIONS:
            here.append(("wT", i))
        jobs += [(w, n) for w, n in here
                 if t is None or w == "wT" or 0 <= t + t_delay(w, n) < B]
    return jobs


def build(nc, x, ctx_in, wq, wk, wv, wo, bo, g, w_q4, w_scale, f_bias, out):
    x_d = x.rearrange("b c n -> (b c) n")
    c_d = ctx_in.rearrange("b c n -> (b c) n")
    out_d = out.rearrange("b c n -> (b c) n")
    q4_d = w_q4.rearrange("(a p g) j -> a p (g j)", p=P, g=NG)
    scale_d = w_scale.rearrange("(a p g) o -> p a (g o)", p=P, g=NG)

    with ExitStack() as stack:
        def sb(name, shape, dt=F32):
            return stack.enter_context(nc.sbuf_tensor(name, shape, dt))

        def psum(name, shape):
            return stack.enter_context(nc.psum_tensor(name, shape, F32))

        def sem(name):
            return stack.enter_context(nc.semaphore(name))

        ident = sb("ident", [P, P])
        ones_r = sb("ones_r", [P, P], F32R)
        wqT_hi, wqT_lo = sb("wqT_hi", [P, HID], F32R), sb("wqT_lo", [P, HID], F32R)
        wkT_hi, wkT_lo = sb("wkT_hi", [P, HID], F32R), sb("wkT_lo", [P, HID], F32R)
        pT = sb("pT", [P, HEADS * P])
        wT_hi = sb("wT_hi", [P, NC, OUT], F32R)
        wT_lo = sb("wT_lo", [P, NC, OUT], F32R)
        bias_bc = sb("bias_bc", [P, OUT])
        bo_c, g_c = sb("bo_c", [P, 1]), sb("g_c", [P, 1])
        g_neg, bg_neg = sb("g_neg", [P, 1]), sb("bg_neg", [P, 1])
        pow_half, eps_c = sb("pow_half", [P, 1]), sb("eps_c", [P, 1])
        xa = sb("xa", [P, N])
        xn_hi, xn_lo = sb("xn_hi", [P, N], F32R), sb("xn_lo", [P, N], F32R)
        cx = sb("cx", [P, N])
        c_hi, c_lo = sb("c_hi", [P, N], F32R), sb("c_lo", [P, N], F32R)
        cT = sb("cT", [P, NC, P])
        ek = sb("ek", [P, N])
        kT = sb("kT", [P, NC, HID])
        qs = sb("qs", [P, 4, HID])
        qT_hi = sb("qT_hi", [P, 2, JC, HALF], F32R)
        qT_lo = sb("qT_lo", [P, 2, JC, HALF], F32R)
        scratch = sb("scratch", [P, N])
        m_s = scratch[:, 0:HID]
        a_n = scratch[:, HID:2 * HID].rearrange("p (j o) -> p j o", j=JC)
        r0 = scratch
        a_hi, a_lo = sb("a_hi", [P, JC, P], F32R), sb("a_lo", [P, JC, P], F32R)
        sq = sb("sq", [P, HALF])
        sq_hi, sq_lo = sb("sq_hi", [P, HALF], F32R), sb("sq_lo", [P, HALF], F32R)
        o1 = sb("o1", [P, N])
        nrm = sb("nrm", [P, N])
        xr = sb("xr", [P, N])
        x1b = sb("x1b", [P, N])
        xT_hi, xT_lo = sb("xT_hi", [P, NC, P], F32R), sb("xT_lo", [P, NC, P], F32R)
        q_max, q_rz = sb("q_max", [P, 2, HEADS]), sb("q_rz", [P, 4, HEADS])
        k_nmax, k_sum = sb("k_nmax", [P, JC]), sb("k_sum", [P, JC])
        k_sum8, k_rz = sb("k_sum8", [P, JC]), sb("k_rz", [P, JC])
        st1, mv1, ve1, rs1 = sb("st1", [P, 12]), sb("mv1", [P, 2]), sb("ve1", [P, 1]), sb("rs1", [P, 1])
        st2, mv2, ve2, rs2 = sb("st2", [P, 12]), sb("mv2", [P, 2]), sb("ve2", [P, 1]), sb("rs2", [P, 1])

        raw = kT
        q4_i = x1b[:, 0:256].bitcast(I32)
        w_i = x1b[:, 256:768].bitcast(I32)
        w_f = x1b[:, 256:768]
        w_s = x1b[:, 768:896].rearrange("p (a g) -> p a g", g=NG)
        w_s2 = x1b[:, 896:1024].rearrange("p (a g) -> p a g", g=NG)
        ones_f = sq[:, 0:P]

        ql = [psum("ql0", [P, HID]), psum("ql1", [P, HID])]
        tb = [psum("tb0", [P, 512]), psum("tb1", [P, 512])]
        kl = psum("kl", [P, N])
        yb = psum("yb", [P, 512])
        ob = psum("ob", [P, 512])

        x_loaded, ctx_loaded, res_loaded, stored = sem("x_loaded"), sem("ctx_loaded"), sem("res_loaded"), sem("stored")
        raw_loaded, small_loaded, q4_loaded = sem("raw_loaded"), sem("small_loaded"), sem("q4_loaded")
        ones_set, ident_set, raw_turned, raw_copied = sem("ones_set"), sem("ident_set"), sem("raw_turned"), sem("raw_copied")
        woT_copied, p_ready, p_copied, smalls_set, s_gneg = sem("woT_copied"), sem("p_ready"), sem("p_copied"), sem("smalls_set"), sem("s_gneg")
        whi_set, w_bits, w_scaled, w_ready, wT_hi_done = sem("whi_set"), sem("w_bits"), sem("w_scaled"), sem("w_ready"), sem("wT_hi_done")
        q_logits, k_logits, m_ready, a_ready = sem("q_logits"), sem("k_logits"), sem("m_ready"), sem("a_ready")
        out_ready, y_ready = sem("out_ready"), sem("y_ready")
        turned = {w: sem(f"{w}_turned") for w in PER}
        taken = {w: sem(f"{w}_taken") for w in PER}
        q_exp, k_exp, qT_hi_done, xn_hi_done, c_hi_done = sem("q_exp"), sem("k_exp"), sem("qT_hi_done"), sem("xn_hi_done"), sem("c_hi_done")
        m_copied, a_hi_done, sq_done, sq_hi_done, o1_done = sem("m_copied"), sem("a_hi_done"), sem("sq_done"), sem("sq_hi_done"), sem("o1_done")
        norm_done, ln_done, r0_done, xT_hi_done = sem("norm_done"), sem("ln_done"), sem("r0_done"), sem("xT_hi_done")
        q_max_done, q_sub, q_sum_done, q_rz_done, k_max_done = sem("q_max_done"), sem("q_sub"), sem("q_sum_done"), sem("q_rz_done"), sem("k_max_done")
        k_sum8_done, k_rz_done, a_scaled, st1_done, mv1_done = sem("k_sum8_done"), sem("k_rz_done"), sem("a_scaled"), sem("st1_done"), sem("mv1_done")
        xn_done, r_done, o_scaled = sem("xn_done"), sem("r_done"), sem("o_scaled")
        st2_done, mv2_done, xn1_done, result = sem("st2_done"), sem("mv2_done"), sem("xn1_done"), sem("result")
        st_seen = sem("st_seen")
        q_scaled, xn_lo_done, c_lo_done, a_lo_done, sq_lo_done = sem("q_scaled"), sem("xn_lo_done"), sem("c_lo_done"), sem("a_lo_done"), sem("sq_lo_done")
        ve1_done, rs1_done, ve2_done, rs2_done, newton, x1_done, x1b_done = (
            sem("ve1_done"), sem("rs1_done"), sem("ve2_done"), sem("rs2_done"), sem("newton"), sem("x1_done"), sem("x1b_done"))

        def wait(eng, semaphore, per, t, delay, n):
            if isinstance(t, int) and t + delay >= B:
                return
            until(eng, semaphore, t * per + (delay * per + n))

        def until(eng, semaphore, value):
            if not isinstance(value, int) or value > 0:
                eng.wait_ge(semaphore, value)

        def live(t, delay):
            return not isinstance(t, int) or 0 <= t + delay < B

        def pipeline(eng, iteration, first):
            for t in range(first, 3):
                iteration(t)
            with eng.Fori(3, B - 2) as t:
                iteration(t)
            for t in range(B - 2, B + 2):
                iteration(t)

        def three_passes(pe, dst, w_hi, w_lo, m_hi, m_lo, start, stop):
            pe.matmul(dst, w_hi, m_hi, start=start, stop=False)
            pe.matmul(dst, w_hi, m_lo, start=False, stop=False)
            return pe.matmul(dst, w_lo, m_hi, start=False, stop=stop)

        block = stack.enter_context(nc.Block())

        @block.sync
        def _(sp):
            sp.dma_start(raw[:, 0, :].rearrange("p (j c) -> p j c", j=JC),
                         wq.rearrange("(j p) c -> p j c", p=P)).then_inc(raw_loaded, 16)
            sp.dma_start(raw[:, 1, :].rearrange("p (j c) -> p j c", j=JC),
                         wk.rearrange("(j p) c -> p j c", p=P)).then_inc(raw_loaded, 16)
            sp.dma_start(raw[:, 2, :].rearrange("p (j c) -> p j c", j=JC),
                         wv.rearrange("(j p) c -> p j c", p=P)).then_inc(raw_loaded, 16)
            sp.dma_start(raw[:, 3, :], wo).then_inc(raw_loaded, 16)
            sp.dma_start(bo_c[:], bo.rearrange("(c o) -> c o", o=1)).then_inc(small_loaded, 16)
            sp.dma_start(g_c[:], g.rearrange("a c o -> (a c) o")).then_inc(small_loaded, 16)
            sp.dma_start(w_s, scale_d).then_inc(small_loaded, 16)
            sp.dma_start(bias_bc[:], f_bias.rearrange("(a n) -> a n", a=1).to_broadcast([P, OUT])).then_inc(small_loaded, 16)

            def iteration(t):
                def value(v):
                    return v if isinstance(v, int) else sp.snap(v)

                row = {d: value((t + d) * P) for d in (1, -1, 2, -2) if live(t, d)}
                x_free, x1_used, c_turned, done = (value(v) for v in (2 * t + 2, t - 1, 2 * t + 4, 2 * t - 2))
                if live(t, 1):
                    until(sp, xn_lo_done, x_free)
                    sp.dma_start(xa[:], x_d[bass.ds(row[1], P), :]).then_inc(x_loaded, 16)
                if live(t, -1):
                    until(sp, x1b_done, x1_used)
                    until(sp, xn1_done, x1_used)
                    sp.dma_start(xr[:], x_d[bass.ds(row[-1], P), :]).then_inc(res_loaded, 16)
                if live(t, 2):
                    until(sp, turned["cT"], c_turned)
                    sp.dma_start(cx[:], c_d[bass.ds(row[2], P), :]).then_inc(ctx_loaded, 16)
                if live(t, -2):
                    until(sp, result, done)
                    sp.dma_start(out_d[bass.ds(row[-2], P), :], x1b[:]).then_inc(stored, 16)

            for t in (-2, -1, 0, 1, 2):
                iteration(t)
            with sp.Fori(3, B - 2) as t:
                iteration(t)
            for t in range(B - 2, B + 2):
                iteration(t)
            sp.wait_ge(stored, 16 * B)

        @block.tensor
        def _(pe):
            pe.wait_ge(ident_set, 1)
            pe.wait_ge(raw_loaded, 64)
            for which, bank in ((0, ql[0]), (1, ql[1]), (3, ob)):
                for j in range(JC):
                    mm = pe.transpose(bank[:, j * P:(j + 1) * P], raw[:, which, j * P:(j + 1) * P], ident[:])
                mm.then_inc(raw_turned, 1)
            pe.wait_ge(woT_copied, 1)
            for h in range(HEADS):
                r = slice(DH * (h % 2), DH * (h % 2) + DH)
                j = slice((h // 2) * P, (h // 2 + 1) * P)
                at = HALF * (h % 2) + P * (h // 2)
                mm = pe.matmul(kl[:, at:at + P], raw[r, 2, j], raw[r, 4, j], start=True, stop=True)
            mm.then_inc(p_ready, 1)
            pe.wait_ge(raw_copied, 2)
            pe.wait_ge(p_copied, 1)

            def iteration(t):
                jobs = t_jobs(t if isinstance(t, int) else None)
                before = []
                if isinstance(t, int):
                    for s in range(-1, t):
                        before += [(s - t, w, n) for w, n in t_jobs(s)]
                else:
                    before = [(-1, w, n) for w, n in t_jobs(None)]
                line = before + [(0, w, n) for w, n in jobs]

                def bank_for(what, n):
                    at = line.index((0, what, n))
                    if at >= 2:
                        back, w, m = line[at - 2]
                        if w == "wT":
                            pe.wait_ge(taken[w], SLOTS * (t + back) + m + 1)
                        else:
                            wait(pe, taken[w], PER[w], t, back + t_delay(w, m), m + 1)
                    return tb[at % 2]

                def turn_q(i, delay):
                    wait(pe, q_scaled, 8, t, delay, i + 1)
                    bank = bank_for("qT", i)
                    for j in range(JC):
                        mm = pe.transpose(bank[:, j * P:(j + 1) * P], qs[:, i % 4, j * P:(j + 1) * P], ident[:])
                    mm.then_inc(turned["qT"], 1)

                def turn_k(j):
                    wait(pe, k_exp, 4, t, 1, j + 1)
                    for half in range(2):
                        bank = bank_for("kT", 2 * j + half)
                        for c in range(4):
                            n = 4 * half + c
                            mm = pe.transpose(bank[:, c * P:(c + 1) * P], ek[:, n * P:(n + 1) * P], ident[:])
                        mm.then_inc(turned["kT"], 1)

                def turn_rows(what, src, halves):
                    for half in halves:
                        bank = bank_for(what, half)
                        for c in range(4):
                            n = 4 * half + c
                            mm = pe.transpose(bank[:, c * P:(c + 1) * P], src[:, n * P:(n + 1) * P], ident[:])
                        mm.then_inc(turned[what], 1)

                def k_logit(j):
                    if j == 0:
                        wait(pe, c_lo_done, 1, t, 1, 1)
                        wait(pe, a_scaled, 2, t, 0, 2)
                    wait(pe, k_exp, 4, t, 1, j)
                    w = slice(j * P, (j + 1) * P)
                    for half in range(2):
                        m = slice(half * HALF, (half + 1) * HALF)
                        mm = three_passes(pe, kl[:, m], wkT_hi[:, w], wkT_lo[:, w], c_hi[:, m], c_lo[:, m], True, True)
                    mm.then_inc(k_logits, 1)

                def ffn(p):
                    half = p // 4
                    if p == 0:
                        wait(pe, taken["xT"], 2, t, -2, 2)
                        wait(pe, result, 2, t, -3, 2)
                        if isinstance(t, int) and t == 2:
                            pe.wait_ge(taken["wT"], 16)
                    if p == 4:
                        wait(pe, result, 2, t, -2, 1)
                    o = slice(half * HALF, (half + 1) * HALF)
                    for c in (2 * (p % 4), 2 * (p % 4) + 1):
                        mm = three_passes(pe, yb[:], xT_hi[:, c, :], xT_lo[:, c, :],
                                          wT_hi[:, c, o], wT_lo[:, c, o], c == 0, c == NC - 1)
                    if p % 4 == 3:
                        mm.then_inc(y_ready, 1)

                def m_part(p):
                    if p == 0:
                        wait(pe, taken["kT"], 8, t, 0, 8)
                        wait(pe, taken["cT"], 2, t, 0, 2)
                        wait(pe, o1_done, 2, t, -1, 1)
                    for c in (2 * p, 2 * p + 1):
                        mm = pe.matmul(ob[:], cT[:, c, :], kT[:, c, :], start=(c == 0), stop=(c == NC - 1))
                    if p == 3:
                        mm.then_inc(m_ready, 1)

                def a_part():
                    wait(pe, m_copied, 1, t, 0, 1)
                    wait(pe, k_exp, 4, t, 0, 4)
                    for j in range(JC):
                        mm = pe.matmul(kl[:, j * 2 * P:(j + 1) * 2 * P], m_s[:, j * P:(j + 1) * P],
                                       pT[:, j * 2 * P:(j + 1) * 2 * P], start=True, stop=True)
                    mm.then_inc(a_ready, 1)

                def out_half(half, delay):
                    if half == 0:
                        wait(pe, taken["qT"], 8, t, delay, 4)
                        wait(pe, a_lo_done, 1, t, delay, 1)
                        wait(pe, o1_done, 2, t, -1, 2)
                    else:
                        wait(pe, taken["qT"], 8, t, delay, 8)
                        wait(pe, m_copied, 1, t, 0, 1)
                    for j in range(JC):
                        mm = three_passes(pe, ob[:], a_hi[:, j, :], a_lo[:, j, :],
                                          qT_hi[:, half, j, :], qT_lo[:, half, j, :], j == 0, j == JC - 1)
                    mm.then_inc(out_ready, 1)

                def squares(half):
                    wait(pe, sq_lo_done, 2, t, -1, half + 1)
                    bank = bank_for("ss", half)
                    pe.matmul(bank[:], ones_r[:], sq_hi[:], start=True, stop=False)
                    pe.matmul(bank[:], ones_r[:], sq_lo[:], start=False, stop=True).then_inc(turned["ss"], 1)

                def q_logit(i, delay):
                    if i % 4 == 0:
                        wait(pe, xn_lo_done, 2, t, delay, 1 + i // 4)
                    wait(pe, q_sub, 8, t, delay, i - 1)
                    r = slice(i * P, (i + 1) * P)
                    three_passes(pe, ql[i % 2][:], xn_hi[:, r], xn_lo[:, r], wqT_hi[:], wqT_lo[:],
                                 True, True).then_inc(q_logits, 1)

                q, q_old, keys, tail, feed = live(t, 0), live(t, -1), live(t, 1), live(t, -1), live(t, -2)
                for i in range(SLOTS):
                    if i == 1 and tail:
                        squares(0)
                    if i == 3 and tail:
                        squares(1)
                    if i < 2 and q_old:
                        turn_q(i + 6, -1)
                    if i >= 2 and q:
                        turn_q(i - 2, 0)
                    if i < 7 and q:
                        q_logit(i + 1, 0)
                    if i == 7 and keys:
                        q_logit(0, 1)
                    if i == 0:
                        for half in range(2):
                            if feed:
                                wait(pe, xn1_done, 1, t, -2, 1)
                                turn_rows("xT", nrm, (half,))
                            if q:
                                m_part(half)
                    if i == 1:
                        if q:
                            m_part(2)
                            m_part(3)
                        if feed:
                            ffn(0)
                    if i == 2:
                        if q_old:
                            out_half(1, -1)
                        if feed:
                            ffn(1)
                        if q:
                            a_part()
                    if i == 3:
                        if feed:
                            ffn(2)
                        if keys:
                            k_logit(0)
                        if feed:
                            ffn(3)
                    if 4 <= i <= 6:
                        if i > 4 and keys:
                            wait(pe, ctx_loaded, 16, t, 1, 16)
                            turn_rows("cT", cx, (i - 5,))
                        if feed:
                            ffn(i)
                        if keys:
                            turn_k(i - 4)
                            k_logit(i - 3)
                    if i == 7:
                        if q:
                            out_half(0, 0)
                        if keys:
                            turn_k(3)
                        if feed:
                            ffn(7)
                    if isinstance(t, int) and t in W_ITERATIONS:
                        pe.wait_ge(w_ready, SLOTS * t + i + 1)
                        bank = bank_for("wT", i)
                        for c in range(4):
                            mm = pe.transpose(bank[:, c * P:(c + 1) * P], w_f[:, c * P:(c + 1) * P], ident[:])
                        mm.then_inc(turned["wT"], 1)

            pipeline(pe, iteration, -1)

        def bank_of(t, what, n):
            if isinstance(t, int):
                at = sum(len(t_jobs(s)) for s in range(-1, t)) + t_jobs(t).index((what, n))
            else:
                at = sum(len(t_jobs(s)) for s in range(-1, 3)) + t_jobs(None).index((what, n))
            return tb[at % 2]

        @block.scalar
        def _(act):
            nc.scalar.preload_act_table_set("natural_log_exp_and_others")
            act.wait_ge(raw_turned, 1)
            nc.scalar.copy(wqT_hi[:], ql[0][:]).then_inc(whi_set, 1)
            act.wait_ge(raw_turned, 2)
            nc.scalar.copy(wkT_hi[:], ql[1][:]).then_inc(whi_set, 1)
            act.wait_ge(raw_turned, 3)
            nc.scalar.copy(raw[:, 4, :], ob[:]).then_inc(woT_copied, 1)
            act.wait_ge(p_ready, 1)
            nc.scalar.copy(pT[:].rearrange("p (j a o) -> p a j o", j=JC, a=2),
                           kl[:].rearrange("p (a j o) -> p a j o", j=JC, a=2)).then_inc(p_copied, 1)
            act.wait_ge(smalls_set, 3)

            def iteration(t):
                q, q_old, keys, tail, feed = live(t, 0), live(t, -1), live(t, 1), live(t, -1), live(t, -2)

                def split_q(i, delay):
                    wait(act, turned["qT"], 8, t, delay, i + 1)
                    if i % 4 == 0:
                        wait(act, out_ready, 2, t, delay - 1, i // 4 + 1)
                    nc.scalar.copy(qT_hi[:, i // 4, :, (i % 4) * P:(i % 4 + 1) * P],
                                   bank_of(t, "qT", i)[:].rearrange("p (j n) -> p j n", j=JC)).then_inc(qT_hi_done, 1)

                def q_exponent(i):
                    wait(act, q_sub, 8, t, 0, i + 1)
                    nc.scalar.activation(qs[:, i % 4, :], qs[:, i % 4, :], ACT.Exp).then_inc(q_exp, 1)

                def k_exponent(j):
                    wait(act, k_max_done, 4, t, 1, j + 1)
                    wait(act, turned["kT"], 8, t, 1, 2 * j)
                    if j == 0:
                        wait(act, k_sum8_done, 1, t, 0, 1)
                    nc.scalar.activation(ek[:], kl[:], ACT.Exp, bias=k_nmax[:, j:j + 1],
                                         accum_out=k_sum[:, j:j + 1]).then_inc(k_exp, 1)

                def copy_k(j):
                    for half in range(2):
                        wait(act, turned["kT"], 8, t, 1, 2 * j + half + 1)
                        if j == 0 and half == 0:
                            wait(act, m_ready, 1, t, 0, 1)
                        nc.scalar.copy(kT[:, 4 * half:4 * half + 4, j * P:(j + 1) * P],
                                       bank_of(t, "kT", 2 * j + half)[:].rearrange("p (c k) -> p c k", c=4)
                                       ).then_inc(taken["kT"], 1)

                def square(half, delay):
                    wait(act, out_ready, 2, t, delay, half + 1)
                    wait(act, sq_lo_done, 2, t, delay, half)
                    nc.scalar.activation(sq[:], ob[:], ACT.Square, bias=bo_c[:]).then_inc(sq_done, 1)

                def leave_out(half, delay):
                    wait(act, turned["ss"], 2, t, delay, half)
                    nc.scalar.activation(sq_hi[:], ob[:], ACT.Square, bias=bo_c[:]).then_inc(sq_hi_done, 1)
                    if half == 0:
                        wait(act, x1_done, 1, t, delay - 1, 1)
                    nc.scalar.activation(o1[:, half * HALF:(half + 1) * HALF], ob[:], ACT.Identity,
                                         bias=bg_neg[:], scale=g_neg[:]).then_inc(o1_done, 1)

                def split_xn(half, delay):
                    h = slice(half * HALF, (half + 1) * HALF)
                    wait(act, xn_done, 2, t, delay, half + 1)
                    wait(act, q_logits, 8, t, delay - 1, 4 * half + 4)
                    nc.scalar.copy(xn_hi[:, h], xa[:, h]).then_inc(xn_hi_done, 1)

                def copy_c(half):
                    wait(act, turned["cT"], 2, t, 1, half + 1)
                    nc.scalar.copy(cT[:, 4 * half:4 * half + 4, :],
                                   bank_of(t, "cT", half)[:].rearrange("p (c k) -> p c k", c=4)
                                   ).then_inc(taken["cT"], 1)

                for i in range(SLOTS):
                    if i == 2 and q:
                        wait(act, m_ready, 1, t, 0, 1)
                        wait(act, r_done, 1, t, -2, 1)
                        nc.scalar.copy(m_s[:], ob[:]).then_inc(m_copied, 1)
                    if i < 2 and q_old:
                        split_q(i + 6, -1)
                    if i >= 2 and q:
                        split_q(i - 2, 0)
                    if i == 3 and q:
                        wait(act, a_scaled, 2, t, 0, 2)
                        wait(act, out_ready, 2, t, -1, 2)
                        nc.scalar.copy(a_hi[:], a_n[:]).then_inc(a_hi_done, 1)
                    if i == 3 and tail:
                        wait(act, taken["ss"], 2, t, -1, 2)
                        nc.scalar.activation(nrm[:], nrm[:], ACT.Sqrt).then_inc(norm_done, 1)
                        nc.scalar.preload_act_table_set("natural_log_exp_and_others")
                    if i >= 4 and keys:
                        k_exponent(i - 4)
                    if 5 <= i <= 6 and keys:
                        copy_c(i - 5)
                    if i == 4 and tail:
                        wait(act, norm_done, 1, t, -1, 1)
                        wait(act, a_ready, 1, t, 0, 1)
                        wait(act, a_lo_done, 1, t, 0, 1)
                        nc.scalar.activation(r0[:], nrm[:], ACT.Ln).then_inc(ln_done, 1)
                    if q:
                        q_exponent(i)
                    if i == 0 and feed:
                        for half in range(2):
                            wait(act, turned["xT"], 2, t, -2, half + 1)
                            if half == 0:
                                wait(act, y_ready, 2, t, -3, 2)
                            nc.scalar.copy(xT_hi[:, 4 * half:4 * half + 4, :],
                                           bank_of(t, "xT", half)[:].rearrange("p (c k) -> p c k", c=4)
                                           ).then_inc(xT_hi_done, 1)
                    if i == 0 and q:
                        split_xn(1, 0)
                    if i == 1 and keys:
                        wait(act, ctx_loaded, 16, t, 1, 16)
                        wait(act, k_logits, 4, t, 0, 4)
                        nc.scalar.copy(c_hi[:], cx[:]).then_inc(c_hi_done, 1)
                    if i == 2 and tail:
                        square(1, -1)
                        leave_out(1, -1)
                    if i == 7 and q:
                        square(0, 0)
                    if i >= 4 and keys:
                        copy_k(i - 4)
                    if i == 7 and q:
                        leave_out(0, 0)
                    if i == 4 and tail:
                        wait(act, ln_done, 1, t, -1, 1)
                        nc.scalar.activation(r0[:], r0[:], ACT.Exp, scale=-1.0).then_inc(r0_done, 1)
                    if i == 5 and keys:
                        split_xn(0, 1)
                    if isinstance(t, int) and t in W_ITERATIONS:
                        u = SLOTS * t + i
                        act.wait_ge(turned["wT"], u + 1)
                        a, wh = u // 2, u % 2
                        nc.scalar.copy(wT_hi[:, 4 * wh:4 * wh + 4, a * P:(a + 1) * P],
                                       bank_of(t, "wT", i)[:].rearrange("p (c k) -> p c k", c=4)).then_inc(wT_hi_done, 1)
                    if isinstance(t, int) and 0 <= SLOTS * t + i + 1 < 2 * OUT // P:
                        u = SLOTS * t + i + 1
                        until(act, w_bits, 2 * u)
                        act.dma_start(q4_i, q4_d[u // 2, :, 256 * (u % 2):256 * (u % 2) + 256]).then_inc(q4_loaded, 16)

            pipeline(act, iteration, -1)

        @block.vector
        def _(dve):
            nc.vector.memset(ones_f, 1.0).then_inc(ones_set, 1)
            nc.vector.memset(pow_half[:], -0.5).then_inc(ones_set, 1)
            nc.vector.memset(eps_c[:], LN_EPS).then_inc(ones_set, 1)
            dve.wait_ge(ones_set, 3)
            nc.vector.tensor_copy(ones_r[:], ones_f).then_inc(smalls_set, 1)
            dve.wait_ge(small_loaded, 64)
            nc.vector.tensor_scalar(g_neg[:], g_c[:], -math.sqrt(C), None, ALU.mult).then_inc(s_gneg, 1)
            nc.vector.tensor_scalar(w_s2, w_s, 2.0 / 15.0, None, ALU.mult).then_inc(smalls_set, 1)
            dve.wait_ge(s_gneg, 1)
            nc.vector.tensor_tensor(bg_neg[:], bo_c[:], g_neg[:], ALU.mult).then_inc(smalls_set, 1)
            dve.wait_ge(whi_set, 1)
            nc.vector.tensor_tensor(wqT_lo[:], ql[0][:], wqT_hi[:], ALU.subtract).then_inc(raw_copied, 1)
            dve.wait_ge(whi_set, 2)
            nc.vector.tensor_tensor(wkT_lo[:], ql[1][:], wkT_hi[:], ALU.subtract).then_inc(raw_copied, 1)
            dve.wait_ge(smalls_set, 3)

            def heads(ap):
                return ap.rearrange("p (h d) -> p h d", h=HEADS)

            def iteration(t):
                q, q_old, keys, tail, feed = live(t, 0), live(t, -1), live(t, 1), live(t, -1), live(t, -2)

                def q_maximum(i):
                    wait(dve, q_logits, 8, t, 0, i + 1)
                    nc.vector.tensor_reduce(q_max[:, i % 2, :], heads(ql[i % 2][:]), AX_X, ALU.max).then_inc(q_max_done, 1)

                def q_subtract(i):
                    wait(dve, q_max_done, 8, t, 0, i + 1)
                    wait(dve, turned["qT"], 8, t, 0, i - 3)
                    nc.vector.tensor_tensor(heads(qs[:, i % 4, :]), heads(ql[i % 2][:]),
                                            q_max[:, i % 2, :].unsqueeze(2).to_broadcast([P, HEADS, DH]),
                                            ALU.subtract).then_inc(q_sub, 1)

                def q_total(i, delay):
                    wait(dve, q_exp, 8, t, delay, i + 1)
                    nc.vector.tensor_reduce(q_rz[:, i % 4, :], heads(qs[:, i % 4, :]), AX_X, ALU.add).then_inc(q_sum_done, 1)

                def q_reciprocal(i, delay):
                    wait(dve, q_sum_done, 8, t, delay, i + 1)
                    nc.vector.reciprocal(q_rz[:, i % 4, :], q_rz[:, i % 4, :]).then_inc(q_rz_done, 1)

                def lo_q(i, delay):
                    at = (slice(None), i // 4, slice(None), slice((i % 4) * P, (i % 4 + 1) * P))
                    wait(dve, qT_hi_done, 8, t, delay, i + 1)
                    nc.vector.tensor_tensor(qT_lo[at], bank_of(t, "qT", i)[:].rearrange("p (j n) -> p j n", j=JC),
                                            qT_hi[at], ALU.subtract).then_inc(taken["qT"], 1)

                def k_maximum(j):
                    wait(dve, k_logits, 4, t, 1, j + 1)
                    nc.vector.tensor_reduce(k_nmax[:, j:j + 1], kl[:], AX_X, ALU.max, negate=True).then_inc(k_max_done, 1)

                def normalise_x(half, delay):
                    h = slice(half * HALF, (half + 1) * HALF)
                    wait(dve, rs1_done, 1, t, delay, 1)
                    nc.vector.tensor_scalar(xa[:, h], xa[:, h], mv1[:, 0:1], rs1[:], ALU.subtract, ALU.mult
                                            ).then_inc(xn_done, 1)

                def copy_squares(half):
                    wait(dve, turned["ss"], 2, t, -1, half + 1)
                    if half == 0:
                        wait(dve, turned["xT"], 2, t, -2, 2)
                    nc.vector.tensor_scalar(nrm[:, half * HALF:(half + 1) * HALF], bank_of(t, "ss", half)[:],
                                            NORM_MIN * NORM_MIN, None, ALU.max).then_inc(taken["ss"], 1)

                def finish(half, delay):
                    h = slice(half * HALF, (half + 1) * HALF)
                    wait(dve, y_ready, 2, t, delay, half + 1)
                    if half == 0:
                        wait(dve, x1b_done, 1, t, delay, 1)
                    nc.vector.tensor_tensor(x1b[:, h], yb[:], x1b[:, h], ALU.add).then_inc(result, 1)

                for i in range(SLOTS):
                    if i == 3 and q:
                        wait(dve, a_ready, 1, t, 0, 1)
                        wait(dve, k_rz_done, 1, t, 0, 1)
                        for head in range(2):
                            r = slice(DH * head, DH * (head + 1))
                            nc.vector.tensor_tensor(
                                a_n[r], kl[r].rearrange("p (j a o) -> p j a o", j=JC, a=2)[:, :, head, :],
                                k_rz[r, :].unsqueeze(2).to_broadcast([DH, JC, P]), ALU.mult).then_inc(a_scaled, 1)
                    if i in (1, 3) and tail:
                        copy_squares(i // 2)
                    if i >= 4 and keys:
                        k_maximum(i - 4)
                    if i == 4 and feed:
                        finish(0, -2)
                    if isinstance(t, int) and t in W_ITERATIONS:
                        u = SLOTS * t + i
                        a, wh = u // 2, u % 2
                        pairs = w_i.rearrange("p (n two) -> p n two", two=2)
                        dve.wait_ge(q4_loaded, 16 * (u + 1))
                        wait(dve, turned["wT"], 1, u, 0, 0)
                        nc.vector.tensor_scalar(pairs[:, :, 0], q4_i, 15, None, ALU.bitwise_and).then_inc(w_bits, 1)
                        nc.vector.tensor_scalar(pairs[:, :, 1], q4_i, 4, 15, ALU.logical_shift_right,
                                                ALU.bitwise_and).then_inc(w_bits, 1)
                    if i == 0 and q_old:
                        q_total(7, -1)
                    if i > 0 and q:
                        q_total(i - 1, 0)
                    if 4 <= i < 7 and q:
                        lo_q(i - 2, 0)
                    if q:
                        q_maximum(i)
                    if i == 0 and q_old:
                        q_reciprocal(7, -1)
                    if i > 0 and q:
                        q_reciprocal(i - 1, 0)
                    if i < 2 and q_old:
                        lo_q(i + 6, -1)
                    if isinstance(t, int) and t in W_ITERATIONS:
                        dve.wait_ge(w_bits, 2 * (u + 1))
                        nc.vector.tensor_tensor(
                            w_f.rearrange("p (g e) -> p g e", e=GROUP), w_i.rearrange("p (g e) -> p g e", e=GROUP),
                            w_s2[:, a, 8 * wh:8 * wh + 8].unsqueeze(2).to_broadcast([P, 8, GROUP]),
                            ALU.mult).then_inc(w_scaled, 1)
                    if q:
                        q_subtract(i)
                    if i == 7 and tail:
                        wait(dve, x1_done, 1, t, -1, 1)
                        for half in range(2):
                            nc.vector.bn_stats(st2[:, 6 * half:6 * half + 6], xr[:, half * HALF:(half + 1) * HALF]).then_inc(st2_done, 1)
                        wait(dve, st2_done, 2, t, -1, 2)
                        dve.sem_inc(st_seen, 1)
                        nc.vector.bn_aggr(mv2[:], st2[:]).then_inc(mv2_done, 1)
                    if i == 7 and q:
                        lo_q(5, 0)
                    if i == 7 and tail:
                        wait(dve, rs2_done, 1, t, -1, 1)
                        nc.vector.tensor_scalar(nrm[:], xr[:], mv2[:, 0:1], rs2[:], ALU.subtract, ALU.mult
                                                ).then_inc(xn1_done, 1)
                    if i == 0 and live(t, -3):
                        finish(1, -3)
                    if i == 0 and q:
                        normalise_x(1, 0)
                    if i == 0 and feed:
                        for half in range(2):
                            at = slice(4 * half, 4 * half + 4)
                            wait(dve, xT_hi_done, 2, t, -2, half + 1)
                            nc.vector.tensor_tensor(xT_lo[:, at, :], bank_of(t, "xT", half)[:].rearrange("p (c k) -> p c k", c=4),
                                                    xT_hi[:, at, :], ALU.subtract).then_inc(taken["xT"], 1)
                    if i == 1 and keys:
                        wait(dve, x_loaded, 16, t, 1, 16)
                        for half in range(2):
                            nc.vector.bn_stats(st1[:, 6 * half:6 * half + 6], xa[:, half * HALF:(half + 1) * HALF]).then_inc(st1_done, 1)
                    if i == 1 and q:
                        wait(dve, k_exp, 4, t, 0, 4)
                        nc.vector.tensor_scalar(k_sum8[:], k_sum[:], math.sqrt(DH), None, ALU.mult).then_inc(k_sum8_done, 1)
                    if i == 1 and keys:
                        wait(dve, st1_done, 2, t, 1, 2)
                        dve.sem_inc(st_seen, 1)
                        nc.vector.bn_aggr(mv1[:], st1[:]).then_inc(mv1_done, 1)
                    if i == 1 and q:
                        wait(dve, k_sum8_done, 1, t, 0, 1)
                        nc.vector.reciprocal(k_rz[:], k_sum8[:]).then_inc(k_rz_done, 1)
                    if i in (2, 3) and q:
                        lo_q(i - 2, 0)
                    if i == 4 and keys:
                        normalise_x(0, 1)
                    if i == 5 and tail:
                        wait(dve, newton, 1, t, -1, 1)
                        nc.vector.scalar_tensor_tensor(out=nrm[:], in0=nrm[:], scalar=-2.0, in1=r0[:],
                                                       op0=ALU.add, op1=ALU.mult).then_inc(r_done, 1)
                    if i == 6 and tail:
                        wait(dve, r_done, 1, t, -1, 1)
                        wait(dve, o1_done, 2, t, -1, 2)
                        nc.vector.tensor_tensor(o1[:], o1[:], nrm[:], ALU.mult).then_inc(o_scaled, 1)
                    if i == 7 and isinstance(t, int) and t == B + 1:
                        finish(1, -2)
                    if isinstance(t, int) and t in W_ITERATIONS:
                        at = (slice(None), slice(4 * wh, 4 * wh + 4), slice(a * P, (a + 1) * P))
                        dve.wait_ge(wT_hi_done, u + 1)
                        nc.vector.tensor_tensor(wT_lo[at], bank_of(t, "wT", i)[:].rearrange("p (c k) -> p c k", c=4),
                                                wT_hi[at], ALU.subtract).then_inc(taken["wT"], 1)

            pipeline(dve, iteration, -1)

        @block.gpsimd
        def _(pool):
            pool.wait_ge(ones_set, 3)
            nc.gpsimd.affine_select(out=ident[:], in_=ones_f, compare_op=ALU.is_equal, fill=0.0, base=0,
                                    pattern=[[-1, P]], channel_multiplier=1).then_inc(ident_set, 1)
            pool.wait_ge(small_loaded, 64)

            def iteration(t):
                q, q_old, keys, tail, feed = live(t, 0), live(t, -1), live(t, 1), live(t, -1), live(t, -2)

                def scale_q(i, delay):
                    wait(pool, q_rz_done, 8, t, delay, i + 1)
                    v = qs[:, i % 4, :].rearrange("p (h d) -> p h d", h=HEADS)
                    nc.gpsimd.tensor_tensor(v, v, q_rz[:, i % 4, :].unsqueeze(2).to_broadcast([P, HEADS, DH]),
                                            ALU.mult).then_inc(q_scaled, 1)

                def lo_xn(half, delay):
                    h = slice(half * HALF, (half + 1) * HALF)
                    wait(pool, xn_hi_done, 2, t, delay, half + 1)
                    nc.gpsimd.tensor_tensor(xn_lo[:, h], xa[:, h], xn_hi[:, h], ALU.subtract).then_inc(xn_lo_done, 1)

                def lo_squares(half, delay):
                    wait(pool, sq_hi_done, 2, t, delay, half + 1)
                    nc.gpsimd.tensor_tensor(sq_lo[:], sq[:], sq_hi[:], ALU.subtract).then_inc(sq_lo_done, 1)

                def deviation(delay, mv_done, mv, ve_done, ve, rs_done, rs):
                    wait(pool, mv_done, 1, t, delay, 1)
                    nc.gpsimd.tensor_tensor(ve[:], mv[:, 1:2], eps_c[:], ALU.add).then_inc(ve_done, 1)
                    wait(pool, ve_done, 1, t, delay, 1)
                    nc.gpsimd.tensor_tensor(rs[:], ve[:], pow_half[:], ALU.pow).then_inc(rs_done, 1)

                for i in range(SLOTS):
                    if i == 5 and tail:
                        wait(pool, r0_done, 1, t, -1, 1)
                        nc.gpsimd.tensor_tensor(nrm[:], nrm[:], r0[:], ALU.mult).then_inc(newton, 1)
                    if i == 0 and q_old:
                        scale_q(7, -1)
                    if i > 0 and q:
                        scale_q(i - 1, 0)
                    if i == 0 and tail:
                        lo_squares(0, -1)
                    if i == 0 and q:
                        lo_xn(1, 0)
                    if i == 1 and keys:
                        wait(pool, c_hi_done, 1, t, 1, 1)
                        nc.gpsimd.tensor_tensor(c_lo[:], cx[:], c_hi[:], ALU.subtract).then_inc(c_lo_done, 1)
                    if i == 1 and feed:
                        wait(pool, stored, 16, t, -3, 16)
                        if isinstance(t, int) and t == 2:
                            pool.wait_ge(turned["wT"], 16)
                        nc.gpsimd.tensor_tensor(x1b[:], xr[:], bias_bc[:], ALU.add).then_inc(x1b_done, 1)
                    if i == 2 and keys:
                        deviation(1, mv1_done, mv1, ve1_done, ve1, rs1_done, rs1)
                    if i == 2 and tail:
                        lo_squares(1, -1)
                    if i == 3 and q:
                        wait(pool, a_hi_done, 1, t, 0, 1)
                        nc.gpsimd.tensor_tensor(a_lo[:], a_n[:], a_hi[:], ALU.subtract).then_inc(a_lo_done, 1)
                    if i == 5 and keys:
                        lo_xn(0, 1)
                    if i == 6 and tail:
                        wait(pool, o_scaled, 1, t, -1, 1)
                        wait(pool, res_loaded, 16, t, -1, 16)
                        nc.gpsimd.tensor_tensor(xr[:], o1[:], xr[:], ALU.add).then_inc(x1_done, 1)
                    if i == 7 and tail:
                        deviation(-1, mv2_done, mv2, ve2_done, ve2, rs2_done, rs2)
                    if isinstance(t, int) and t in W_ITERATIONS:
                        u = SLOTS * t + i
                        a, wh = u // 2, u % 2
                        pool.wait_ge(w_scaled, u + 1)
                        v = w_f.rearrange("p (g e) -> p g e", e=GROUP)
                        nc.gpsimd.tensor_tensor(v, v, w_s[:, a, 8 * wh:8 * wh + 8].unsqueeze(2).to_broadcast([P, 8, GROUP]),
                                                ALU.subtract).then_inc(w_ready, 1)

            pipeline(pool, iteration, -1)


_INS = ["x", "ctx_4096", "L0_xattn_Wq", "L0_xattn_Wk", "L0_xattn_Wv", "L0_xattn_Wo", "L0_xattn_bo", "L0_xattn_g",
        "L0_ffn_weight_q4", "L0_ffn_weight_scale", "L0_ffn_bias"]


def kernel(**inputs):
    import numpy as _np
    import concourse.bacc as _bacc
    from concourse import mybir as _mybir
    from concourse.bass_utils import run_bass_kernel_spmd as _run

    nc = _bacc.Bacc("TRN2", target_bir_lowering=False, num_devices=1)
    arrays, args = {}, []
    for name in _INS:
        a = _np.ascontiguousarray(inputs[name])
        arrays[f"in_{name}_dram"] = a
        args.append(nc.dram_tensor(f"in_{name}_dram", a.shape, _mybir.dt.from_np(a.dtype), kind="ExternalInput").ap())
    args.append(nc.dram_tensor("out_0_dram", (B, C, N), _mybir.dt.float32, kind="ExternalOutput").ap())
    build(nc, *args)
    r = _run(nc, [arrays], core_ids=[0])
    return r.results[0]["out_0_dram"]
```

```python
from contextlib import ExitStack
import math

import concourse.bass as bass
from concourse import mybir

F32 = mybir.dt.float32
F32R = mybir.dt.float32r
I32 = mybir.dt.int32
ALU = mybir.AluOpType
ACT = mybir.ActivationFunctionType
AX_X = mybir.AxisListType.X

B, C, N = 32, 128, 1024
HEADS, DH = 8, 64
HID = HEADS * DH
P = 128
NC = N // P
JC = HID // P
HALF = N // 2
OUT, GROUP = 1024, 64
NG = N // GROUP
LN_EPS = 1e-5
NORM_MIN = 1e-12
SLOTS = NC

T_ORDER = [
    [("qT", 6), ("xT", 0), ("xT", 1)],
    [("ss", 0), ("qT", 7)],
    [("qT", 0)],
    [("ss", 1), ("qT", 1)],
    [("qT", 2), ("kT", 0), ("kT", 1)],
    [("qT", 3), ("cT", 0), ("kT", 2), ("kT", 3)],
    [("qT", 4), ("cT", 1), ("kT", 4), ("kT", 5)],
    [("qT", 5), ("kT", 6), ("kT", 7)],
]
PER = {"qT": 8, "ss": 2, "kT": 8, "cT": 2, "xT": 2, "wT": 1}
UNITS = 2 * OUT // P
W_UNITS = {-1: (0, 0, 0, 0, 2, 2, 2, 2), 0: (1, 1, 1, 1, 1, 1, 1, 1)}


def units_of(t, i):
    if not isinstance(t, int) or t not in W_UNITS:
        return []
    done = sum(sum(W_UNITS[s]) for s in W_UNITS if s < t) + sum(W_UNITS[t][:i])
    return list(range(done, done + W_UNITS[t][i]))


def t_delay(what, n):
    return {"qT": 0 if n < 6 else -1, "ss": -1, "kT": 1, "cT": 1, "xT": -2, "wT": 0}[what]


def t_jobs(t):
    jobs = []
    for i, slot in enumerate(T_ORDER):
        here = [("wT", u) for u in units_of(t, i)] + list(slot)
        jobs += [(w, n) for w, n in here
                 if t is None or w == "wT" or 0 <= t + t_delay(w, n) < B]
    return jobs


def build(nc, x, ctx_in, wq, wk, wv, wo, bo, g, w_q4, w_scale, f_bias, out):
    x_d = x.rearrange("b c n -> (b c) n")
    c_d = ctx_in.rearrange("b c n -> (b c) n")
    out_d = out.rearrange("b c n -> (b c) n")
    q4_d = w_q4.rearrange("(a p g) j -> a p (g j)", p=P, g=NG)
    scale_d = w_scale.rearrange("(a p g) o -> p a (g o)", p=P, g=NG)

    with ExitStack() as stack:
        def sb(name, shape, dt=F32):
            return stack.enter_context(nc.sbuf_tensor(name, shape, dt))

        def psum(name, shape):
            return stack.enter_context(nc.psum_tensor(name, shape, F32))

        def sem(name):
            return stack.enter_context(nc.semaphore(name))

        ident = sb("ident", [P, P])
        ones_r = sb("ones_r", [P, P], F32R)
        wqT_hi, wqT_lo = sb("wqT_hi", [P, HID], F32R), sb("wqT_lo", [P, HID], F32R)
        wkT_hi, wkT_lo = sb("wkT_hi", [P, HID], F32R), sb("wkT_lo", [P, HID], F32R)
        pT = sb("pT", [P, HEADS * P])
        wT_hi = sb("wT_hi", [P, NC, OUT], F32R)
        wT_lo = sb("wT_lo", [P, NC, OUT], F32R)
        bias_bc = sb("bias_bc", [P, OUT])
        bo_c, g_c = sb("bo_c", [P, 1]), sb("g_c", [P, 1])
        g_neg, bg_neg = sb("g_neg", [P, 1]), sb("bg_neg", [P, 1])
        pow_half, eps_c = sb("pow_half", [P, 1]), sb("eps_c", [P, 1])
        xa = sb("xa", [P, N])
        xn_hi, xn_lo = sb("xn_hi", [P, N], F32R), sb("xn_lo", [P, N], F32R)
        cx = sb("cx", [P, N])
        c_hi, c_lo = sb("c_hi", [P, N], F32R), sb("c_lo", [P, N], F32R)
        cT = sb("cT", [P, NC, P])
        ek = sb("ek", [P, N])
        kT = sb("kT", [P, NC, HID])
        qs = sb("qs", [P, 4, HID])
        qT_hi = sb("qT_hi", [P, 2, JC, HALF], F32R)
        qT_lo = sb("qT_lo", [P, 2, JC, HALF], F32R)
        scratch = sb("scratch", [P, N])
        m_s = scratch[:, 0:HID]
        a_n = scratch[:, HID:2 * HID].rearrange("p (j o) -> p j o", j=JC)
        r0 = scratch
        a_hi, a_lo = sb("a_hi", [P, JC, P], F32R), sb("a_lo", [P, JC, P], F32R)
        sq = sb("sq", [P, HALF])
        sq_hi, sq_lo = sb("sq_hi", [P, HALF], F32R), sb("sq_lo", [P, HALF], F32R)
        o1 = sb("o1", [P, N])
        nrm = sb("nrm", [P, N])
        xr = sb("xr", [P, N])
        x1b = sb("x1b", [P, N])
        xT_hi, xT_lo = sb("xT_hi", [P, NC, P], F32R), sb("xT_lo", [P, NC, P], F32R)
        q_max, q_rz = sb("q_max", [P, 2, HEADS]), sb("q_rz", [P, 4, HEADS])
        k_nmax, k_sum = sb("k_nmax", [P, JC]), sb("k_sum", [P, JC])
        k_sum8, k_rz = sb("k_sum8", [P, JC]), sb("k_rz", [P, JC])
        st1, mv1, ve1, rs1 = sb("st1", [P, 12]), sb("mv1", [P, 2]), sb("ve1", [P, 1]), sb("rs1", [P, 1])
        st2, mv2, ve2, rs2 = sb("st2", [P, 12]), sb("mv2", [P, 2]), sb("ve2", [P, 1]), sb("rs2", [P, 1])

        raw = kT
        q4_i = [xr[:, 256 * k:256 * k + 256].bitcast(I32) for k in range(4)]
        w_i = [nrm[:, 512 * k:512 * k + 512].bitcast(I32) for k in range(2)]
        w_f = [nrm[:, 512 * k:512 * k + 512] for k in range(2)]
        w_s = x1b[:, 768:896].rearrange("p (a g) -> p a g", g=NG)
        w_s2 = x1b[:, 896:1024].rearrange("p (a g) -> p a g", g=NG)
        ones_f = sq[:, 0:P]

        ql = [psum("ql0", [P, HID]), psum("ql1", [P, HID])]
        tb = [psum("tb0", [P, 512]), psum("tb1", [P, 512])]
        kl = psum("kl", [P, N])
        yb = psum("yb", [P, 512])
        ob = psum("ob", [P, 512])

        x_loaded, ctx_loaded = sem("x_loaded"), sem("ctx_loaded")
        res_loaded, stored = sem("res_loaded"), sem("stored")
        raw_loaded, small_loaded = [sem(f"raw_loaded{k}") for k in range(4)], sem("small_loaded")
        q4_loaded = [sem(f"q4_loaded{k}") for k in range(4)]
        ones_set, ident_set = sem("ones_set"), sem("ident_set")
        raw_turned, raw_copied = sem("raw_turned"), sem("raw_copied")
        woT_copied, p_ready, p_copied = sem("woT_copied"), sem("p_ready"), sem("p_copied")
        smalls_set, s_gneg = sem("smalls_set"), sem("s_gneg")
        whi_set, w_bits, w_scaled = sem("whi_set"), sem("w_bits"), sem("w_scaled")
        w_ready, wT_hi_done = sem("w_ready"), sem("wT_hi_done")
        q_logits, k_logits, m_ready, a_ready = sem("q_logits"), sem("k_logits"), sem("m_ready"), sem("a_ready")
        out_ready, y_ready = sem("out_ready"), sem("y_ready")
        turned = {w: sem(f"{w}_turned") for w in PER}
        taken = {w: sem(f"{w}_taken") for w in PER}
        q_exp, k_exp, qT_hi_done = sem("q_exp"), sem("k_exp"), sem("qT_hi_done")
        xn_hi_done, c_hi_done = sem("xn_hi_done"), sem("c_hi_done")
        m_copied, a_hi_done, sq_done = sem("m_copied"), sem("a_hi_done"), sem("sq_done")
        sq_hi_done, o1_done = sem("sq_hi_done"), sem("o1_done")
        norm_done, ln_done, r0_done, xT_hi_done = sem("norm_done"), sem("ln_done"), sem("r0_done"), sem("xT_hi_done")
        q_max_done, q_sub, q_sum_done = sem("q_max_done"), sem("q_sub"), sem("q_sum_done")
        q_rz_done, k_max_done = sem("q_rz_done"), sem("k_max_done")
        k_sum8_done, k_rz_done, a_scaled = sem("k_sum8_done"), sem("k_rz_done"), sem("a_scaled")
        st1_done, mv1_done = sem("st1_done"), sem("mv1_done")
        xn_done, r_done, o_scaled = sem("xn_done"), sem("r_done"), sem("o_scaled")
        st2_done, mv2_done, xn1_done, result = sem("st2_done"), sem("mv2_done"), sem("xn1_done"), sem("result")
        st_seen = sem("st_seen")
        q_scaled, xn_lo_done, c_lo_done = sem("q_scaled"), sem("xn_lo_done"), sem("c_lo_done")
        a_lo_done, sq_lo_done = sem("a_lo_done"), sem("sq_lo_done")
        ve1_done, rs1_done, ve2_done, rs2_done, newton, x1_done, x1b_done = (
            sem("ve1_done"), sem("rs1_done"), sem("ve2_done"), sem("rs2_done"), sem("newton"), sem("x1_done"), sem("x1b_done"))

        def wait(eng, semaphore, per, t, delay, n):
            if isinstance(t, int) and t + delay >= B:
                return
            until(eng, semaphore, t * per + (delay * per + n))

        def until(eng, semaphore, value):
            if not isinstance(value, int) or value > 0:
                eng.wait_ge(semaphore, value)

        y_banks = (yb[:], kl[:, 0:HALF])

        def y_bank(batch, half):
            return y_banks[half if isinstance(batch, int) and batch == B - 1 else 0]

        def last(t):
            return isinstance(t, int) and t == B

        def c_slot(t):
            return 0 if isinstance(t, int) and t < 0 else 1

        def next_units(t, i):
            return [] if not isinstance(t, int) else units_of(t, i + 1) if i + 1 < SLOTS else units_of(t + 1, 0)

        def live(t, delay):
            return not isinstance(t, int) or 0 <= t + delay < B

        def pipeline(eng, iteration, first):
            for t in range(first, 3):
                iteration(t)
            with eng.Fori(3, B - 2) as t:
                iteration(t)
            for t in range(B - 2, B + 2):
                iteration(t)

        def load_unit(eng, u):
            at = slice(256 * (u % 2), 256 * (u % 2) + 256)
            eng.dma_start(q4_i[u % 4], q4_d[u // 2, :, at]).then_inc(q4_loaded[u % 4], 16)

        def three_passes(pe, dst, w_hi, w_lo, m_hi, m_lo, start, stop):
            pe.matmul(dst, w_hi, m_hi, start=start, stop=False)
            pe.matmul(dst, w_hi, m_lo, start=False, stop=False)
            return pe.matmul(dst, w_lo, m_hi, start=False, stop=stop)

        block = stack.enter_context(nc.Block())

        @block.sync
        def _(sp):
            for k, w in ((1, wk), (3, wo), (0, wq), (2, wv)):
                if k == 3:
                    sp.dma_start(raw[:, k, :], w).then_inc(raw_loaded[k], 16)
                else:
                    sp.dma_start(raw[:, k, :].rearrange("p (j c) -> p j c", j=JC),
                                 w.rearrange("(j p) c -> p j c", p=P)).then_inc(raw_loaded[k], 16)
            sp.dma_start(cx[:], c_d[0:P, :]).then_inc(ctx_loaded, 16)
            sp.dma_start(w_s, scale_d).then_inc(small_loaded, 16)
            sp.dma_start(bo_c[:], bo.rearrange("(c o) -> c o", o=1)).then_inc(small_loaded, 16)
            sp.dma_start(g_c[:], g.rearrange("a c o -> (a c) o")).then_inc(small_loaded, 16)
            sp.dma_start(bias_bc[:], f_bias.rearrange("(a n) -> a n", a=1).to_broadcast([P, OUT])).then_inc(small_loaded, 16)
            sp.dma_start(xa[:], x_d[0:P, :]).then_inc(x_loaded, 16)
            for u in range(4):
                load_unit(sp, u)

            def iteration(t):
                def value(v):
                    return v if isinstance(v, int) else sp.snap(v)

                row = {d: value((t + d) * P) for d in (1, -1, 2, -2) if live(t, d)}
                x_free, x1_used, c_turned, done = (value(v) for v in (2 * t + 2, t - 1, 2 * t + 4, 2 * t - 2))
                if live(t, 1) and not (isinstance(t, int) and t == -1):
                    until(sp, xn_lo_done, x_free)
                    sp.dma_start(xa[:], x_d[bass.ds(row[1], P), :]).then_inc(x_loaded, 16)
                if live(t, -1):
                    if isinstance(t, int) and t == 1:
                        until(sp, w_bits, 2 * UNITS)
                    until(sp, x1b_done, x1_used)
                    until(sp, xn1_done, x1_used)
                    sp.dma_start(xr[:], x_d[bass.ds(row[-1], P), :]).then_inc(res_loaded, 16)
                if live(t, 2):
                    until(sp, turned["cT"], c_turned)
                    sp.dma_start(cx[:], c_d[bass.ds(row[2], P), :]).then_inc(ctx_loaded, 16)
                if live(t, -2):
                    until(sp, result, done)
                    sp.dma_start(out_d[bass.ds(row[-2], P), :], x1b[:]).then_inc(stored, 16)

            for t in (-1, 0, 1, 2):
                iteration(t)
            with sp.Fori(3, B - 2) as t:
                iteration(t)
            for t in range(B - 2, B + 2):
                iteration(t)
            sp.wait_ge(stored, 16 * B)

        @block.tensor
        def _(pe):
            pe.wait_ge(ident_set, 1)
            for which, bank in ((1, ql[1]), (3, ob), (0, ql[0])):
                pe.wait_ge(raw_loaded[which], 16)
                for j in range(JC):
                    mm = pe.transpose(bank[:, j * P:(j + 1) * P], raw[:, which, j * P:(j + 1) * P], ident[:])
                mm.then_inc(raw_turned, 1)
            pe.wait_ge(raw_loaded[2], 16)
            pe.wait_ge(woT_copied, 1)
            for h in range(HEADS):
                r = slice(DH * (h % 2), DH * (h % 2) + DH)
                j = slice((h // 2) * P, (h // 2 + 1) * P)
                bank = (ob, yb)[h % 2]
                mm = pe.matmul(bank[:, j], raw[r, 2, j], raw[r, 4, j], start=True, stop=True)
            mm.then_inc(p_ready, 1)
            pe.wait_ge(raw_copied, 2)

            def iteration(t):
                jobs = t_jobs(t if isinstance(t, int) else None)
                before = []
                if isinstance(t, int):
                    for s in range(-1, t):
                        before += [(s - t, w, n) for w, n in t_jobs(s)]
                else:
                    before = [(-1, w, n) for w, n in t_jobs(None)]
                line = before + [(0, w, n) for w, n in jobs]

                def bank_for(what, n):
                    at = line.index((0, what, n))
                    if at >= 2:
                        back, w, m = line[at - 2]
                        if w == "wT":
                            pe.wait_ge(taken[w], m + 1)
                        else:
                            wait(pe, taken[w], PER[w], t, back + t_delay(w, m), m + 1)
                    return tb[at % 2]

                def turn_q(i, delay):
                    wait(pe, q_scaled, 8, t, delay, i + 1)
                    bank = bank_for("qT", i)
                    for j in range(JC):
                        mm = pe.transpose(bank[:, j * P:(j + 1) * P], qs[:, i % 4, j * P:(j + 1) * P], ident[:])
                    mm.then_inc(turned["qT"], 1)

                def turn_k(j):
                    wait(pe, k_exp, 4, t, 1, j + 1)
                    for half in range(2):
                        bank = bank_for("kT", 2 * j + half)
                        for c in range(4):
                            n = 4 * half + c
                            mm = pe.transpose(bank[:, c * P:(c + 1) * P], ek[:, n * P:(n + 1) * P], ident[:])
                        mm.then_inc(turned["kT"], 1)

                def turn_rows(what, src, halves):
                    for half in halves:
                        bank = bank_for(what, half)
                        for c in range(4):
                            n = 4 * half + c
                            mm = pe.transpose(bank[:, c * P:(c + 1) * P], src[:, n * P:(n + 1) * P], ident[:])
                        mm.then_inc(turned[what], 1)

                def k_logit(j):
                    if j == 0:
                        wait(pe, c_lo_done, 1, t, 1, 1)
                        wait(pe, a_scaled, 2, t, 0, 2)
                    wait(pe, k_exp, 4, t, 1, j)
                    w = slice(j * P, (j + 1) * P)
                    for half in range(2):
                        m = slice(half * HALF, (half + 1) * HALF)
                        mm = three_passes(pe, kl[:, m], wkT_hi[:, w], wkT_lo[:, w], c_hi[:, m], c_lo[:, m], True, True)
                    mm.then_inc(k_logits, 1)

                def ffn(p):
                    half = p // 4
                    if p % 2 == 0 and p < 4:
                        wait(pe, taken["xT"], 2, t, -2, p // 2 + 1)
                    if p == 0:
                        wait(pe, result, 2, t, -3, 2)
                        if isinstance(t, int) and t == 2:
                            pe.wait_ge(taken["wT"], UNITS)
                    if p == 4 and y_bank(t - 2, 0) is y_bank(t - 2, 1):
                        wait(pe, result, 2, t, -2, 1)
                    o = slice(half * HALF, (half + 1) * HALF)
                    for c in (2 * (p % 4), 2 * (p % 4) + 1):
                        mm = three_passes(pe, y_bank(t - 2, half), xT_hi[:, c, :], xT_lo[:, c, :],
                                          wT_hi[:, c, o], wT_lo[:, c, o], c == 0, c == NC - 1)
                    if p % 4 == 3:
                        mm.then_inc(y_ready, 1)

                def m_part(p):
                    if p == 0 and isinstance(t, int) and t == 0:
                        pe.wait_ge(p_copied, 2)
                    if p == 0:
                        wait(pe, taken["kT"], 8, t, 0, 8)
                        wait(pe, taken["cT"], 2, t, 0, 2)
                        wait(pe, o1_done, 2, t, -1, 1)
                    for c in (2 * p, 2 * p + 1):
                        mm = pe.matmul(ob[:], cT[:, c, :], kT[:, c, :], start=(c == 0), stop=(c == NC - 1))
                    if p == 3:
                        mm.then_inc(m_ready, 1)

                def a_part():
                    wait(pe, m_copied, 1, t, 0, 1)
                    wait(pe, k_exp, 4, t, 0, 4)
                    for j in range(JC):
                        mm = pe.matmul(kl[:, j * 2 * P:(j + 1) * 2 * P], m_s[:, j * P:(j + 1) * P],
                                       pT[:, j * 2 * P:(j + 1) * 2 * P], start=True, stop=True)
                    mm.then_inc(a_ready, 1)

                def out_half(half, delay):
                    if half == 0:
                        wait(pe, taken["qT"], 8, t, delay, 4)
                        wait(pe, a_lo_done, 1, t, delay, 1)
                        wait(pe, o1_done, 2, t, -1, 2)
                    else:
                        wait(pe, taken["qT"], 8, t, delay, 8)
                        wait(pe, m_copied, 1, t, 0, 1)
                    for j in range(JC):
                        mm = three_passes(pe, ob[:], a_hi[:, j, :], a_lo[:, j, :],
                                          qT_hi[:, half, j, :], qT_lo[:, half, j, :], j == 0, j == JC - 1)
                    mm.then_inc(out_ready, 1)

                def squares(half):
                    wait(pe, sq_lo_done, 2, t, -1, half + 1)
                    bank = bank_for("ss", half)
                    pe.matmul(bank[:], ones_r[:], sq_hi[:], start=True, stop=False)
                    pe.matmul(bank[:], ones_r[:], sq_lo[:], start=False, stop=True).then_inc(turned["ss"], 1)

                def q_logit(i, delay):
                    if i % 4 == 0:
                        wait(pe, xn_lo_done, 2, t, delay, 1 + i // 4)
                    wait(pe, q_sub, 8, t, delay, i - 1)
                    r = slice(i * P, (i + 1) * P)
                    three_passes(pe, ql[i % 2][:], xn_hi[:, r], xn_lo[:, r], wqT_hi[:], wqT_lo[:],
                                 True, True).then_inc(q_logits, 1)

                q, q_old, keys, tail, feed = live(t, 0), live(t, -1), live(t, 1), live(t, -1), live(t, -2)
                for i in range(SLOTS):
                    for u in units_of(t, i):
                        pe.wait_ge(w_ready, u + 1)
                        bank = bank_for("wT", u)
                        for c in range(4):
                            mm = pe.transpose(bank[:, c * P:(c + 1) * P], w_f[u % 2][:, c * P:(c + 1) * P], ident[:])
                        mm.then_inc(turned["wT"], 1)
                    if i == 1 and q:
                        m_part(2)
                    if i == 1 and tail:
                        squares(0)
                    if i == 3 and tail:
                        squares(1)
                    if i < 2 and q_old:
                        turn_q(i + 6, -1)
                    if i >= 2 and q:
                        turn_q(i - 2, 0)
                    if i < 7 and q:
                        q_logit(i + 1, 0)
                    if i == 7 and keys:
                        q_logit(0, 1)
                    if i == 0:
                        for half in range(2):
                            if q:
                                m_part(half)
                            if feed:
                                wait(pe, xn1_done, 1, t, -2, 1)
                                turn_rows("xT", nrm, (half,))
                    if i == 1:
                        if q:
                            m_part(3)
                        if feed:
                            ffn(0)
                    if i == 2:
                        if q_old:
                            out_half(1, -1)
                        if feed:
                            ffn(1)
                        if q:
                            a_part()
                    if i == 3:
                        if feed:
                            ffn(2)
                        if keys:
                            k_logit(0)
                        if feed:
                            ffn(3)
                    if 4 <= i <= 6:
                        if i > 4 and keys:
                            wait(pe, ctx_loaded, 16, t, 1, 16)
                            turn_rows("cT", cx, (i - 5,))
                        if feed:
                            ffn(i)
                        if keys:
                            turn_k(i - 4)
                            k_logit(i - 3)
                    if i == 7:
                        if q:
                            out_half(0, 0)
                        if keys:
                            turn_k(3)
                        if feed:
                            ffn(7)

            pipeline(pe, iteration, -1)

        def bank_of(t, what, n):
            if isinstance(t, int):
                at = sum(len(t_jobs(s)) for s in range(-1, t)) + t_jobs(t).index((what, n))
            else:
                at = sum(len(t_jobs(s)) for s in range(-1, 3)) + t_jobs(None).index((what, n))
            return tb[at % 2]

        @block.scalar
        def _(act):
            nc.scalar.preload_act_table_set("natural_log_exp_and_others")
            act.wait_ge(raw_turned, 1)
            nc.scalar.copy(wkT_hi[:], ql[1][:]).then_inc(whi_set, 1)
            act.wait_ge(raw_turned, 2)
            nc.scalar.copy(raw[:, 4, :], ob[:]).then_inc(woT_copied, 1)
            act.wait_ge(raw_turned, 3)
            nc.scalar.copy(wqT_hi[:], ql[0][:]).then_inc(whi_set, 1)
            act.wait_ge(smalls_set, 3)

            def iteration(t):
                q, q_old, keys, tail, feed = live(t, 0), live(t, -1), live(t, 1), live(t, -1), live(t, -2)

                def split_q(i, delay):
                    wait(act, turned["qT"], 8, t, delay, i + 1)
                    if i % 4 == 0:
                        wait(act, out_ready, 2, t, delay - 1, i // 4 + 1)
                    nc.scalar.copy(qT_hi[:, i // 4, :, (i % 4) * P:(i % 4 + 1) * P],
                                   bank_of(t, "qT", i)[:].rearrange("p (j n) -> p j n", j=JC)).then_inc(qT_hi_done, 1)

                def q_exponent(i):
                    wait(act, q_sub, 8, t, 0, i + 1)
                    nc.scalar.activation(qs[:, i % 4, :], qs[:, i % 4, :], ACT.Exp).then_inc(q_exp, 1)

                def k_exponent(j):
                    wait(act, k_max_done, 4, t, 1, j + 1)
                    wait(act, turned["kT"], 8, t, 1, 2 * j)
                    if j == 0:
                        wait(act, k_sum8_done, 1, t, 0, 1)
                    nc.scalar.activation(ek[:], kl[:], ACT.Exp, bias=k_nmax[:, j:j + 1],
                                         accum_out=k_sum[:, j:j + 1]).then_inc(k_exp, 1)

                def copy_k(j):
                    for half in range(2):
                        wait(act, turned["kT"], 8, t, 1, 2 * j + half + 1)
                        if j == 0 and half == 0:
                            wait(act, m_ready, 1, t, 0, 1)
                        nc.scalar.copy(kT[:, 4 * half:4 * half + 4, j * P:(j + 1) * P],
                                       bank_of(t, "kT", 2 * j + half)[:].rearrange("p (c k) -> p c k", c=4)
                                       ).then_inc(taken["kT"], 1)

                def square(half, delay):
                    wait(act, out_ready, 2, t, delay, half + 1)
                    wait(act, sq_lo_done, 2, t, delay, half)
                    nc.scalar.activation(sq[:], ob[:], ACT.Square, bias=bo_c[:]).then_inc(sq_done, 1)

                def leave_out(half, delay):
                    wait(act, turned["ss"], 2, t, delay, half)
                    nc.scalar.activation(sq_hi[:], ob[:], ACT.Square, bias=bo_c[:]).then_inc(sq_hi_done, 1)
                    if half == 0:
                        wait(act, x1_done, 1, t, delay - 1, 1)
                    nc.scalar.activation(o1[:, half * HALF:(half + 1) * HALF], ob[:], ACT.Identity,
                                         bias=bg_neg[:], scale=g_neg[:]).then_inc(o1_done, 1)

                def split_xn(half, delay):
                    h = slice(half * HALF, (half + 1) * HALF)
                    wait(act, xn_done, 2, t, delay, half + 1)
                    wait(act, q_logits, 8, t, delay - 1, 4 * half + 4)
                    nc.scalar.copy(xn_hi[:, h], xa[:, h]).then_inc(xn_hi_done, 1)

                def copy_c(half):
                    wait(act, turned["cT"], 2, t, 1, half + 1)
                    nc.scalar.copy(cT[:, 4 * half:4 * half + 4, :],
                                   bank_of(t, "cT", half)[:].rearrange("p (c k) -> p c k", c=4)
                                   ).then_inc(taken["cT"], 1)

                for i in range(SLOTS):
                    for u in units_of(t, i):
                        a, wh = u // 2, u % 2
                        act.wait_ge(turned["wT"], u + 1)
                        nc.scalar.copy(wT_hi[:, 4 * wh:4 * wh + 4, a * P:(a + 1) * P],
                                       bank_of(t, "wT", u)[:].rearrange("p (c k) -> p c k", c=4)).then_inc(wT_hi_done, 1)
                        if u + 4 < UNITS:
                            act.wait_ge(w_bits, 2 * (u + 1))
                            load_unit(act, u + 4)
                    if i == 2 and q:
                        wait(act, m_ready, 1, t, 0, 1)
                        wait(act, r_done, 1, t, -2, 1)
                        nc.scalar.copy(m_s[:], ob[:]).then_inc(m_copied, 1)
                    if i < 2 and q_old:
                        split_q(i + 6, -1)
                    if i >= 2 and q:
                        split_q(i - 2, 0)
                    if i == 3 and q:
                        wait(act, a_scaled, 2, t, 0, 2)
                        wait(act, out_ready, 2, t, -1, 2)
                        nc.scalar.copy(a_hi[:], a_n[:]).then_inc(a_hi_done, 1)
                    if i == 3 and q and not keys:
                        q_exponent(3)
                    if i == 3 and tail:
                        wait(act, taken["ss"], 2, t, -1, 2)
                        nc.scalar.activation(nrm[:], nrm[:], ACT.Sqrt).then_inc(norm_done, 1)
                        nc.scalar.preload_act_table_set("natural_log_exp_and_others")
                    if i >= 4 and keys:
                        k_exponent(i - 4)
                    if 5 <= i <= 6 and keys:
                        copy_c(i - 5)
                    if i == 4 and tail:
                        wait(act, norm_done, 1, t, -1, 1)
                        wait(act, a_ready, 1, t, 0, 1)
                        wait(act, a_lo_done, 1, t, 0, 1)
                        nc.scalar.activation(r0[:], nrm[:], ACT.Ln).then_inc(ln_done, 1)
                    if i in (5, 6) and keys:
                        copy_k(i - 4)
                    if i == c_slot(t) and keys:
                        wait(act, ctx_loaded, 16, t, 1, 16)
                        wait(act, k_logits, 4, t, 0, 4)
                        nc.scalar.copy(c_hi[:], cx[:]).then_inc(c_hi_done, 1)
                    if q and (i != 3 or keys):
                        q_exponent(i)
                    if i == 0 and feed:
                        for half in range(2):
                            wait(act, turned["xT"], 2, t, -2, half + 1)
                            if half == 0:
                                wait(act, y_ready, 2, t, -3, 2)
                            nc.scalar.copy(xT_hi[:, 4 * half:4 * half + 4, :],
                                           bank_of(t, "xT", half)[:].rearrange("p (c k) -> p c k", c=4)
                                           ).then_inc(xT_hi_done, 1)
                    if i == 0 and q:
                        split_xn(1, 0)
                    if i == 0 and isinstance(t, int) and t == -1:
                        act.wait_ge(p_ready, 1)
                        for a, bank in enumerate((ob, yb)):
                            nc.scalar.copy(pT[:].rearrange("p (j a o) -> p j a o", j=JC, a=2)[:, :, a, :],
                                           bank[:].rearrange("p (j o) -> p j o", j=JC)).then_inc(p_copied, 1)
                    if i == 2 and tail:
                        square(1, -1)
                        leave_out(1, -1)
                    if i == 7 and q:
                        square(0, 0)
                    if i in (4, 7) and keys:
                        copy_k(i - 4)
                    if i == 7 and q:
                        leave_out(0, 0)
                    if i == 4 and tail:
                        wait(act, ln_done, 1, t, -1, 1)
                        nc.scalar.activation(r0[:], r0[:], ACT.Exp, scale=-1.0).then_inc(r0_done, 1)
                    if i == 5 and keys:
                        split_xn(0, 1)

            pipeline(act, iteration, -1)

        @block.vector
        def _(dve):
            nc.vector.memset(ones_f, 1.0).then_inc(ones_set, 1)
            nc.vector.memset(pow_half[:], -0.5).then_inc(ones_set, 1)
            nc.vector.memset(eps_c[:], LN_EPS).then_inc(ones_set, 1)
            dve.wait_ge(ones_set, 3)
            nc.vector.tensor_copy(ones_r[:], ones_f).then_inc(smalls_set, 1)
            dve.wait_ge(whi_set, 1)
            nc.vector.tensor_tensor(wkT_lo[:], ql[1][:], wkT_hi[:], ALU.subtract).then_inc(raw_copied, 1)
            dve.wait_ge(whi_set, 2)
            nc.vector.tensor_tensor(wqT_lo[:], ql[0][:], wqT_hi[:], ALU.subtract).then_inc(raw_copied, 1)
            dve.wait_ge(small_loaded, 64)
            nc.vector.tensor_scalar(g_neg[:], g_c[:], -math.sqrt(C), None, ALU.mult).then_inc(s_gneg, 1)
            nc.vector.tensor_scalar(w_s2, w_s, 2.0 / 15.0, None, ALU.mult).then_inc(smalls_set, 1)
            dve.wait_ge(s_gneg, 1)
            nc.vector.tensor_tensor(bg_neg[:], bo_c[:], g_neg[:], ALU.mult).then_inc(smalls_set, 1)
            dve.wait_ge(smalls_set, 3)

            def heads(ap):
                return ap.rearrange("p (h d) -> p h d", h=HEADS)

            def unpack(u):
                pairs = w_i[u % 2].rearrange("p (n two) -> p n two", two=2)
                dve.wait_ge(q4_loaded[u % 4], 16 * (u // 4 + 1))
                until(dve, turned["wT"], u - 1)
                nc.vector.tensor_scalar(pairs[:, :, 0], q4_i[u % 4], 15, None, ALU.bitwise_and).then_inc(w_bits, 1)
                nc.vector.tensor_scalar(pairs[:, :, 1], q4_i[u % 4], 4, 15, ALU.logical_shift_right,
                                        ALU.bitwise_and).then_inc(w_bits, 1)

            def scale(u):
                dve.wait_ge(w_bits, 2 * (u + 1))
                a, at = u // 2, slice(8 * (u % 2), 8 * (u % 2) + 8)
                nc.vector.tensor_tensor(
                    w_f[u % 2].rearrange("p (g e) -> p g e", e=GROUP), w_i[u % 2].rearrange("p (g e) -> p g e", e=GROUP),
                    w_s2[:, a, at].unsqueeze(2).to_broadcast([P, 8, GROUP]), ALU.mult).then_inc(w_scaled, 1)

            def split_w(t, u):
                a, wh = u // 2, u % 2
                at = (slice(None), slice(4 * wh, 4 * wh + 4), slice(a * P, (a + 1) * P))
                dve.wait_ge(wT_hi_done, u + 1)
                nc.vector.tensor_tensor(wT_lo[at], bank_of(t, "wT", u)[:].rearrange("p (c k) -> p c k", c=4),
                                        wT_hi[at], ALU.subtract).then_inc(taken["wT"], 1)

            def iteration(t):
                q, q_old, keys, tail, feed = live(t, 0), live(t, -1), live(t, 1), live(t, -1), live(t, -2)

                def q_maximum(i):
                    wait(dve, q_logits, 8, t, 0, i + 1)
                    nc.vector.tensor_reduce(q_max[:, i % 2, :], heads(ql[i % 2][:]), AX_X, ALU.max).then_inc(q_max_done, 1)

                def q_subtract(i):
                    wait(dve, q_max_done, 8, t, 0, i + 1)
                    wait(dve, turned["qT"], 8, t, 0, i - 3)
                    nc.vector.tensor_tensor(heads(qs[:, i % 4, :]), heads(ql[i % 2][:]),
                                            q_max[:, i % 2, :].unsqueeze(2).to_broadcast([P, HEADS, DH]),
                                            ALU.subtract).then_inc(q_sub, 1)

                def q_total(i, delay):
                    wait(dve, q_exp, 8, t, delay, i + 1)
                    nc.vector.tensor_reduce(q_rz[:, i % 4, :], heads(qs[:, i % 4, :]), AX_X, ALU.add).then_inc(q_sum_done, 1)

                def q_reciprocal(i, delay):
                    wait(dve, q_sum_done, 8, t, delay, i + 1)
                    nc.vector.reciprocal(q_rz[:, i % 4, :], q_rz[:, i % 4, :]).then_inc(q_rz_done, 1)

                def lo_q(i, delay):
                    at = (slice(None), i // 4, slice(None), slice((i % 4) * P, (i % 4 + 1) * P))
                    wait(dve, qT_hi_done, 8, t, delay, i + 1)
                    nc.vector.tensor_tensor(qT_lo[at], bank_of(t, "qT", i)[:].rearrange("p (j n) -> p j n", j=JC),
                                            qT_hi[at], ALU.subtract).then_inc(taken["qT"], 1)

                def k_maximum(j):
                    wait(dve, k_logits, 4, t, 1, j + 1)
                    nc.vector.tensor_reduce(k_nmax[:, j:j + 1], kl[:], AX_X, ALU.max, negate=True).then_inc(k_max_done, 1)

                def normalise_x(half, delay):
                    h = slice(half * HALF, (half + 1) * HALF)
                    wait(dve, rs1_done, 1, t, delay, 1)
                    nc.vector.tensor_scalar(xa[:, h], xa[:, h], mv1[:, 0:1], rs1[:], ALU.subtract, ALU.mult
                                            ).then_inc(xn_done, 1)

                def copy_squares(half):
                    wait(dve, turned["ss"], 2, t, -1, half + 1)
                    if half == 0:
                        wait(dve, turned["xT"], 2, t, -2, 2)
                    nc.vector.tensor_scalar(nrm[:, half * HALF:(half + 1) * HALF], bank_of(t, "ss", half)[:],
                                            NORM_MIN * NORM_MIN, None, ALU.max).then_inc(taken["ss"], 1)

                def finish(half, delay):
                    h = slice(half * HALF, (half + 1) * HALF)
                    wait(dve, y_ready, 2, t, delay, half + 1)
                    if half == 0:
                        wait(dve, x1b_done, 1, t, delay, 1)
                    nc.vector.tensor_tensor(x1b[:, h], y_bank(t + delay, half), x1b[:, h], ALU.add).then_inc(result, 1)

                for i in range(SLOTS):
                    if i == 3 and q:
                        wait(dve, a_ready, 1, t, 0, 1)
                        wait(dve, k_rz_done, 1, t, 0, 1)
                        for head in range(2):
                            r = slice(DH * head, DH * (head + 1))
                            nc.vector.tensor_tensor(
                                a_n[r], kl[r].rearrange("p (j a o) -> p j a o", j=JC, a=2)[:, :, head, :],
                                k_rz[r, :].unsqueeze(2).to_broadcast([DH, JC, P]), ALU.mult).then_inc(a_scaled, 1)
                    if i == 3 and last(t):
                        wait(dve, sq_hi_done, 2, t, -1, 2)
                        nc.vector.tensor_tensor(sq_lo[:], sq[:], sq_hi[:], ALU.subtract).then_inc(sq_lo_done, 1)
                    if i in (1, 3) and tail:
                        copy_squares(i // 2)
                    if i >= 4 and keys:
                        k_maximum(i - 4)
                    for u in units_of(t, i):
                        split_w(t, u)
                    if i == 4 and feed:
                        finish(0, -2)
                    if i == 0 and q_old:
                        q_total(7, -1)
                    if i > 0 and q:
                        q_total(i - 1, 0)
                    if 4 <= i < 7 and q and keys:
                        lo_q(i - 2, 0)
                    if q:
                        q_maximum(i)
                    if i == 0 and q_old:
                        q_reciprocal(7, -1)
                    if i > 0 and q:
                        q_reciprocal(i - 1, 0)
                    if i < 2 and q_old:
                        lo_q(i + 6, -1)
                    if q:
                        q_subtract(i)
                    for u in next_units(t, i):
                        unpack(u)
                        scale(u)
                    if i == 7 and q:
                        lo_q(5, 0)
                    if i == 7 and tail:
                        wait(dve, x1_done, 1, t, -1, 1)
                        for half in range(2):
                            nc.vector.bn_stats(st2[:, 6 * half:6 * half + 6], xr[:, half * HALF:(half + 1) * HALF]).then_inc(st2_done, 1)
                        wait(dve, st2_done, 2, t, -1, 2)
                        dve.sem_inc(st_seen, 1)
                        nc.vector.bn_aggr(mv2[:], st2[:]).then_inc(mv2_done, 1)
                    if i == 7 and tail:
                        wait(dve, rs2_done, 1, t, -1, 1)
                        nc.vector.tensor_scalar(nrm[:], xr[:], mv2[:, 0:1], rs2[:], ALU.subtract, ALU.mult
                                                ).then_inc(xn1_done, 1)
                    if i == 0 and live(t, -3):
                        finish(1, -3)
                    if i == 0 and q:
                        normalise_x(1, 0)
                    if i == 0 and feed:
                        for half in range(2):
                            at = slice(4 * half, 4 * half + 4)
                            wait(dve, xT_hi_done, 2, t, -2, half + 1)
                            nc.vector.tensor_tensor(xT_lo[:, at, :], bank_of(t, "xT", half)[:].rearrange("p (c k) -> p c k", c=4),
                                                    xT_hi[:, at, :], ALU.subtract).then_inc(taken["xT"], 1)
                    if i == 1 and keys:
                        wait(dve, x_loaded, 16, t, 1, 16)
                        for half in range(2):
                            nc.vector.bn_stats(st1[:, 6 * half:6 * half + 6], xa[:, half * HALF:(half + 1) * HALF]).then_inc(st1_done, 1)
                    if i == 1 and q:
                        wait(dve, k_exp, 4, t, 0, 4)
                        nc.vector.tensor_scalar(k_sum8[:], k_sum[:], math.sqrt(DH), None, ALU.mult).then_inc(k_sum8_done, 1)
                    if i == 1 and keys:
                        wait(dve, st1_done, 2, t, 1, 2)
                        dve.sem_inc(st_seen, 1)
                        nc.vector.bn_aggr(mv1[:], st1[:]).then_inc(mv1_done, 1)
                    if i == 1 and q:
                        wait(dve, k_sum8_done, 1, t, 0, 1)
                        nc.vector.reciprocal(k_rz[:], k_sum8[:]).then_inc(k_rz_done, 1)
                    if q and (i in (2, 3) or 4 <= i < 7 and not keys):
                        lo_q(i - 2, 0)
                    if i == 4 and keys:
                        normalise_x(0, 1)
                    if i == 5 and tail and not keys:
                        wait(dve, r0_done, 1, t, -1, 1)
                        nc.vector.tensor_tensor(nrm[:], nrm[:], r0[:], ALU.mult).then_inc(newton, 1)
                    if i == 5 and tail:
                        wait(dve, newton, 1, t, -1, 1)
                        nc.vector.scalar_tensor_tensor(out=nrm[:], in0=nrm[:], scalar=-2.0, in1=r0[:],
                                                       op0=ALU.add, op1=ALU.mult).then_inc(r_done, 1)
                    if i == 6 and tail:
                        wait(dve, r_done, 1, t, -1, 1)
                        wait(dve, o1_done, 2, t, -1, 2)
                        nc.vector.tensor_tensor(o1[:], o1[:], nrm[:], ALU.mult).then_inc(o_scaled, 1)
                    if i == 6 and last(t):
                        wait(dve, o_scaled, 1, t, -1, 1)
                        wait(dve, res_loaded, 16, t, -1, 16)
                        nc.vector.tensor_tensor(xr[:], o1[:], xr[:], ALU.add).then_inc(x1_done, 1)
                    if i == 7 and isinstance(t, int) and t == B + 1:
                        finish(1, -2)

            pipeline(dve, iteration, -1)

        @block.gpsimd
        def _(pool):
            pool.wait_ge(ones_set, 3)
            nc.gpsimd.affine_select(out=ident[:], in_=ones_f, compare_op=ALU.is_equal, fill=0.0, base=0,
                                    pattern=[[-1, P]], channel_multiplier=1).then_inc(ident_set, 1)
            pool.wait_ge(small_loaded, 64)

            def less_scale(u):
                a, at = u // 2, slice(8 * (u % 2), 8 * (u % 2) + 8)
                pool.wait_ge(w_scaled, u + 1)
                v = w_f[u % 2].rearrange("p (g e) -> p g e", e=GROUP)
                nc.gpsimd.tensor_tensor(v, v, w_s[:, a, at].unsqueeze(2).to_broadcast([P, 8, GROUP]),
                                        ALU.subtract).then_inc(w_ready, 1)

            def iteration(t):
                q, q_old, keys, tail, feed = live(t, 0), live(t, -1), live(t, 1), live(t, -1), live(t, -2)

                def scale_q(i, delay):
                    wait(pool, q_rz_done, 8, t, delay, i + 1)
                    v = qs[:, i % 4, :].rearrange("p (h d) -> p h d", h=HEADS)
                    nc.gpsimd.tensor_tensor(v, v, q_rz[:, i % 4, :].unsqueeze(2).to_broadcast([P, HEADS, DH]),
                                            ALU.mult).then_inc(q_scaled, 1)

                def lo_xn(half, delay):
                    h = slice(half * HALF, (half + 1) * HALF)
                    wait(pool, xn_hi_done, 2, t, delay, half + 1)
                    nc.gpsimd.tensor_tensor(xn_lo[:, h], xa[:, h], xn_hi[:, h], ALU.subtract).then_inc(xn_lo_done, 1)

                def lo_squares(half, delay):
                    wait(pool, sq_hi_done, 2, t, delay, half + 1)
                    nc.gpsimd.tensor_tensor(sq_lo[:], sq[:], sq_hi[:], ALU.subtract).then_inc(sq_lo_done, 1)

                def deviation(delay, mv_done, mv, ve_done, ve, rs_done, rs):
                    wait(pool, mv_done, 1, t, delay, 1)
                    nc.gpsimd.tensor_tensor(ve[:], mv[:, 1:2], eps_c[:], ALU.add).then_inc(ve_done, 1)
                    wait(pool, ve_done, 1, t, delay, 1)
                    nc.gpsimd.tensor_tensor(rs[:], ve[:], pow_half[:], ALU.pow).then_inc(rs_done, 1)

                for i in range(SLOTS):
                    if i == 5 and tail and keys:
                        wait(pool, r0_done, 1, t, -1, 1)
                        nc.gpsimd.tensor_tensor(nrm[:], nrm[:], r0[:], ALU.mult).then_inc(newton, 1)
                    if i == 0 and q_old:
                        scale_q(7, -1)
                    if i > 0 and q:
                        scale_q(i - 1, 0)
                    for u in next_units(t, i):
                        less_scale(u)
                    if i == 0 and tail:
                        lo_squares(0, -1)
                    if i == 0 and q:
                        lo_xn(1, 0)
                    if i == c_slot(t) and keys:
                        wait(pool, c_hi_done, 1, t, 1, 1)
                        nc.gpsimd.tensor_tensor(c_lo[:], cx[:], c_hi[:], ALU.subtract).then_inc(c_lo_done, 1)
                    if i == 1 and feed:
                        wait(pool, stored, 16, t, -3, 16)
                        nc.gpsimd.tensor_tensor(x1b[:], xr[:], bias_bc[:], ALU.add).then_inc(x1b_done, 1)
                    if i == 2 and tail and not last(t):
                        lo_squares(1, -1)
                    if i == 2 and keys:
                        deviation(1, mv1_done, mv1, ve1_done, ve1, rs1_done, rs1)
                    if i == 3 and q:
                        wait(pool, a_hi_done, 1, t, 0, 1)
                        nc.gpsimd.tensor_tensor(a_lo[:], a_n[:], a_hi[:], ALU.subtract).then_inc(a_lo_done, 1)
                    if i == 5 and keys:
                        lo_xn(0, 1)
                    if i == 6 and tail and not last(t):
                        wait(pool, o_scaled, 1, t, -1, 1)
                        wait(pool, res_loaded, 16, t, -1, 16)
                        nc.gpsimd.tensor_tensor(xr[:], o1[:], xr[:], ALU.add).then_inc(x1_done, 1)
                    if i == 7 and tail:
                        deviation(-1, mv2_done, mv2, ve2_done, ve2, rs2_done, rs2)

            pipeline(pool, iteration, -1)


_INS = ["x", "ctx_4096", "L0_xattn_Wq", "L0_xattn_Wk", "L0_xattn_Wv", "L0_xattn_Wo", "L0_xattn_bo", "L0_xattn_g",
        "L0_ffn_weight_q4", "L0_ffn_weight_scale", "L0_ffn_bias"]


def kernel(**inputs):
    import numpy as _np
    import concourse.bacc as _bacc
    from concourse import mybir as _mybir
    from concourse.bass_utils import run_bass_kernel_spmd as _run

    nc = _bacc.Bacc("TRN2", target_bir_lowering=False, num_devices=1)
    arrays, args = {}, []
    for name in _INS:
        a = _np.ascontiguousarray(inputs[name])
        arrays[f"in_{name}_dram"] = a
        args.append(nc.dram_tensor(f"in_{name}_dram", a.shape, _mybir.dt.from_np(a.dtype), kind="ExternalInput").ap())
    args.append(nc.dram_tensor("out_0_dram", (B, C, N), _mybir.dt.float32, kind="ExternalOutput").ap())
    build(nc, *args)
    r = _run(nc, [arrays], core_ids=[0])
    return r.results[0]["out_0_dram"]
```
